# Optimizing a Trainium2 kernel written in Bass

```python
import numpy as np
import jax
import jax.numpy as jnp

def _softmax(x, axis=-1):
    return jax.nn.softmax(x, axis=axis)

def _gelu(x):
    return jax.nn.gelu(x, approximate=True)

def _silu(x):
    return jax.nn.silu(x)

def _sigmoid(x):
    return jax.nn.sigmoid(x)

def _layernorm(x, axis=-1, eps=1e-05):
    m = jnp.mean(x, axis=axis, keepdims=True)
    v = jnp.var(x, axis=axis, keepdims=True)
    return (x - m) / jnp.sqrt(v + eps)

def _scatter_add(tgt, idx, src, axis=0):
    return tgt.at[idx].add(src)

def _segment_sum(src, seg, n):
    return jax.ops.segment_sum(src, seg, n)
kernel_name = 'mk_xattn_seq_d4_seqx_r8_501109'

def setup_inputs(seed: int=0):
    np.random.seed(seed)
    _w = jnp.asarray

    def _rec_inputs():
        import jax
        import jax.numpy as jnp
        _rk = jax.random.key(seed)
        x = -0.0002928 + 1 * jax.random.normal(jax.random.fold_in(_rk, 1), (32, 128, 128), jnp.float32)
        _lenS = 128 - jax.random.randint(jax.random.fold_in(_rk, 7), (32,), 0, max(1, 128 // 4) + 1, jnp.int32)
        _lenS2 = 128 - jax.random.randint(jax.random.fold_in(_rk, 8), (32,), 0, max(1, 128 // 4) + 1, jnp.int32)
        _ctx_768P = jax.random.normal(jax.random.fold_in(_rk, 11), (32, 16, 96), jnp.float32)
        _ctx_768c = jax.random.dirichlet(jax.random.fold_in(_rk, 511), 0.3 * jnp.ones((16,), jnp.float32), (32, 128))
        _ctx_768t = jnp.einsum('bsk,bkd->bsd', _ctx_768c, _ctx_768P)
        _ctx_768t = _ctx_768t * jax.lax.rsqrt(jnp.mean(jnp.square(_ctx_768t)) + 1e-12) * 0.953939
        ctx_768 = 0.000651243 + 0.998673 * (_ctx_768t + 0.3 * jax.random.normal(jax.random.fold_in(_rk, 611), (32, 128, 96), jnp.float32))
        return (x, ctx_768)
    x, ctx_768 = _rec_inputs()

    def _L0_xattn_setup():
        import jax, jax.numpy as jnp
        import numpy as np
        DIM = 128
        H = 16
        DH = 64
        CTX_DIM = 96
        INNER_FF = 4 * DIM
        SCALE = DH ** (-0.5)
        EPS = 1e-05

        def layer_norm(x, g, b):
            mu = jnp.mean(x, axis=-1, keepdims=True)
            var = jnp.var(x, axis=-1, keepdims=True)
            return (x - mu) * jax.lax.rsqrt(var + EPS) * g + b

        def attention(x, ctx, Wq, Wk, Wv, Wo, bo):
            b, n, _ = x.shape
            m = ctx.shape[1]
            q = (x @ Wq).reshape(b, n, H, DH)
            k = (ctx @ Wk).reshape(b, m, H, DH)
            v = (ctx @ Wv).reshape(b, m, H, DH)
            sim = jnp.einsum('bihd,bjhd->bhij', q, k) * SCALE
            attn = jax.nn.softmax(sim, axis=-1)
            out = jnp.einsum('bhij,bjhd->bihd', attn, v).reshape(b, n, H * DH)
            return out @ Wo + bo
        key = jax.random.key(seed)
        ks = jax.random.split(key, 16)
        s = 0.02
        inp = {'x': jax.random.normal(ks[0], (4, 128, DIM), jnp.float32), 'context': jax.random.normal(ks[1], (4, 77, CTX_DIM), jnp.float32), 'ln1_g': jnp.ones((DIM,), jnp.float32), 'ln1_b': jnp.zeros((DIM,), jnp.float32), 'Wq1': s * jax.random.normal(ks[2], (DIM, H * DH), jnp.float32), 'Wk1': s * jax.random.normal(ks[3], (DIM, H * DH), jnp.float32), 'Wv1': s * jax.random.normal(ks[4], (DIM, H * DH), jnp.float32), 'Wo1': s * jax.random.normal(ks[5], (H * DH, DIM), jnp.float32), 'bo1': jnp.zeros((DIM,), jnp.float32), 'ln2_g': jnp.ones((DIM,), jnp.float32), 'ln2_b': jnp.zeros((DIM,), jnp.float32), 'Wq2': s * jax.random.normal(ks[6], (DIM, H * DH), jnp.float32), 'Wk2': s * jax.random.normal(ks[7], (CTX_DIM, H * DH), jnp.float32), 'Wv2': s * jax.random.normal(ks[8], (CTX_DIM, H * DH), jnp.float32), 'Wo2': s * jax.random.normal(ks[9], (H * DH, DIM), jnp.float32), 'bo2': jnp.zeros((DIM,), jnp.float32), 'ln3_g': jnp.ones((DIM,), jnp.float32), 'ln3_b': jnp.zeros((DIM,), jnp.float32), 'Wp': s * jax.random.normal(ks[10], (DIM, 2 * INNER_FF), jnp.float32), 'bp': jnp.zeros((2 * INNER_FF,), jnp.float32), 'Wf2': s * jax.random.normal(ks[11], (INNER_FF, DIM), jnp.float32), 'bf2': jnp.zeros((DIM,), jnp.float32)}
        return inp
    _L0_xattn_all = _L0_xattn_setup()
    _L0_xattn_in = {k: v for k, v in _L0_xattn_all.items() if k in ('ln1_g', 'ln1_b', 'Wq1', 'Wk1', 'Wv1', 'Wo1', 'bo1', 'ln2_g', 'ln2_b', 'Wq2', 'Wk2', 'Wv2', 'Wo2', 'bo2', 'ln3_g', 'ln3_b', 'Wp', 'bp', 'Wf2', 'bf2')}
    del _L0_xattn_all

    def _L1_xattn_setup():
        import jax, jax.numpy as jnp
        import numpy as np
        LATENT = 128
        TEXT = 96
        HEADS = 16
        HEAD_DIM = LATENT // HEADS
        SCALE = HEAD_DIM ** (-0.5)
        LN_EPS = 1e-05
        key = jax.random.key(seed)
        ks = jax.random.split(key, 16)
        B, Tx, Txf = (4, 512, 32)

        def lin(k, fan_in, fan_out):
            bound = 1.0 / np.sqrt(fan_in)
            kw, kb = jax.random.split(k)
            W = jax.random.uniform(kw, (fan_in, fan_out), jnp.float32, -bound, bound)
            b = jax.random.uniform(kb, (fan_out,), jnp.float32, -bound, bound)
            return (W, b)
        Wq, bq = lin(ks[0], LATENT, LATENT)
        Wk, bk = lin(ks[1], TEXT, LATENT)
        Wv, bv = lin(ks[2], TEXT, LATENT)
        Wo, bo = lin(ks[3], LATENT, LATENT)
        W1, b1 = lin(ks[4], LATENT, 4 * LATENT)
        W2, b2 = lin(ks[5], 4 * LATENT, LATENT)
        return {'x': jax.random.normal(ks[6], (B, Tx, LATENT), jnp.float32), 'xf': jax.random.normal(ks[7], (B, Txf, TEXT), jnp.float32), 'Wq': Wq, 'bq': bq, 'Wk': Wk, 'bk': bk, 'Wv': Wv, 'bv': bv, 'Wo': Wo, 'bo': bo, 'ln_g': jnp.ones((LATENT,), jnp.float32), 'ln_b': jnp.zeros((LATENT,), jnp.float32), 'W1': W1, 'b1': b1, 'W2': W2, 'b2': b2}
    _L1_xattn_all = _L1_xattn_setup()
    _L1_xattn_in = {k: v for k, v in _L1_xattn_all.items() if k in ('Wq', 'bq', 'Wk', 'bk', 'Wv', 'bv', 'Wo', 'bo', 'ln_g', 'ln_b', 'W1', 'b1', 'W2', 'b2')}
    del _L1_xattn_all

    def _L2_xattn_setup():
        import jax, jax.numpy as jnp
        import numpy as np
        D_Q, D_CTX, N_HEADS, HEAD_DIM = (128, 96, 16, 64)
        INNER = N_HEADS * HEAD_DIM
        EPS = 1e-05

        def _layernorm(x, gamma, beta):
            mu = jnp.mean(x, axis=-1, keepdims=True)
            var = jnp.var(x, axis=-1, keepdims=True)
            return (x - mu) * jax.lax.rsqrt(var + EPS) * gamma + beta
        key = jax.random.key(seed)
        ks = jax.random.split(key, 8)
        B, NQ, NC = (4, 128, 128)
        s_q = 1.0 / np.sqrt(D_Q)
        s_c = 1.0 / np.sqrt(D_CTX)
        s_i = 1.0 / np.sqrt(INNER)
        return {'x': jax.random.normal(ks[0], (B, NQ, D_Q), jnp.float32), 'context': jax.random.normal(ks[1], (B, NC, D_CTX), jnp.float32), 'Wq': jax.random.normal(ks[2], (D_Q, INNER), jnp.float32) * s_q, 'Wk': jax.random.normal(ks[3], (D_CTX, INNER), jnp.float32) * s_c, 'Wv': jax.random.normal(ks[4], (D_CTX, INNER), jnp.float32) * s_c, 'Wo': jax.random.normal(ks[5], (INNER, D_Q), jnp.float32) * s_i, 'bo': jnp.zeros((D_Q,), jnp.float32), 'gamma': jnp.ones((D_Q,), jnp.float32), 'beta': jnp.zeros((D_Q,), jnp.float32)}
    _L2_xattn_all = _L2_xattn_setup()
    _L2_xattn_in = {k: v for k, v in _L2_xattn_all.items() if k in ('Wq', 'Wk', 'Wv', 'Wo', 'bo', 'gamma', 'beta')}
    del _L2_xattn_all

    def _L3_xattn_setup():
        import jax, jax.numpy as jnp
        import numpy as np
        DIM = 128
        CTX_DIM = 96
        HEADS = 16
        HEAD_DIM = DIM // HEADS
        key = jax.random.key(seed)
        ks = jax.random.split(key, 8)
        B, L, Lc = (2, 256, 128)
        x = jax.random.normal(ks[0], (B, L, DIM), dtype=jnp.float32)
        context = jax.random.normal(ks[1], (B, Lc, CTX_DIM), dtype=jnp.float32)
        Wq = jax.random.normal(ks[2], (DIM, DIM), dtype=jnp.float32) * (1.0 / np.sqrt(DIM))
        Wk = jax.random.normal(ks[3], (DIM, CTX_DIM), dtype=jnp.float32) * (1.0 / np.sqrt(CTX_DIM))
        Wv = jax.random.normal(ks[4], (DIM, CTX_DIM), dtype=jnp.float32) * (1.0 / np.sqrt(CTX_DIM))
        Wo = jax.random.normal(ks[5], (DIM, DIM), dtype=jnp.float32) * (1.0 / np.sqrt(DIM))
        bo = jax.random.normal(ks[6], (DIM,), dtype=jnp.float32) * 0.01
        return {'x': x, 'context': context, 'Wq': Wq, 'Wk': Wk, 'Wv': Wv, 'Wo': Wo, 'bo': bo}
    _L3_xattn_all = _L3_xattn_setup()
    _L3_xattn_in = {k: v for k, v in _L3_xattn_all.items() if k in ('Wq', 'Wk', 'Wv', 'Wo', 'bo')}
    del _L3_xattn_all
    return {'x': x, 'ctx_768': ctx_768, 'L0_xattn_ln1_g': _L0_xattn_in['ln1_g'], 'L0_xattn_ln1_b': _L0_xattn_in['ln1_b'], 'L0_xattn_Wq1': _L0_xattn_in['Wq1'], 'L0_xattn_Wk1': _L0_xattn_in['Wk1'], 'L0_xattn_Wv1': _L0_xattn_in['Wv1'], 'L0_xattn_Wo1': _L0_xattn_in['Wo1'], 'L0_xattn_bo1': _L0_xattn_in['bo1'], 'L0_xattn_ln2_g': _L0_xattn_in['ln2_g'], 'L0_xattn_ln2_b': _L0_xattn_in['ln2_b'], 'L0_xattn_Wq2': _L0_xattn_in['Wq2'], 'L0_xattn_Wk2': _L0_xattn_in['Wk2'], 'L0_xattn_Wv2': _L0_xattn_in['Wv2'], 'L0_xattn_Wo2': _L0_xattn_in['Wo2'], 'L0_xattn_bo2': _L0_xattn_in['bo2'], 'L0_xattn_ln3_g': _L0_xattn_in['ln3_g'], 'L0_xattn_ln3_b': _L0_xattn_in['ln3_b'], 'L0_xattn_Wp': _L0_xattn_in['Wp'], 'L0_xattn_bp': _L0_xattn_in['bp'], 'L0_xattn_Wf2': _L0_xattn_in['Wf2'], 'L0_xattn_bf2': _L0_xattn_in['bf2'], 'L1_xattn_Wq': _L1_xattn_in['Wq'], 'L1_xattn_bq': _L1_xattn_in['bq'], 'L1_xattn_Wk': _L1_xattn_in['Wk'], 'L1_xattn_bk': _L1_xattn_in['bk'], 'L1_xattn_Wv': _L1_xattn_in['Wv'], 'L1_xattn_bv': _L1_xattn_in['bv'], 'L1_xattn_Wo': _L1_xattn_in['Wo'], 'L1_xattn_bo': _L1_xattn_in['bo'], 'L1_xattn_ln_g': _L1_xattn_in['ln_g'], 'L1_xattn_ln_b': _L1_xattn_in['ln_b'], 'L1_xattn_W1': _L1_xattn_in['W1'], 'L1_xattn_b1': _L1_xattn_in['b1'], 'L1_xattn_W2': _L1_xattn_in['W2'], 'L1_xattn_b2': _L1_xattn_in['b2'], 'L2_xattn_Wq': _L2_xattn_in['Wq'], 'L2_xattn_Wk': _L2_xattn_in['Wk'], 'L2_xattn_Wv': _L2_xattn_in['Wv'], 'L2_xattn_Wo': _L2_xattn_in['Wo'], 'L2_xattn_bo': _L2_xattn_in['bo'], 'L2_xattn_gamma': _L2_xattn_in['gamma'], 'L2_xattn_beta': _L2_xattn_in['beta'], 'L3_xattn_Wq': _L3_xattn_in['Wq'], 'L3_xattn_Wk': _L3_xattn_in['Wk'], 'L3_xattn_Wv': _L3_xattn_in['Wv'], 'L3_xattn_Wo': _L3_xattn_in['Wo'], 'L3_xattn_bo': _L3_xattn_in['bo']}

def reference(x, ctx_768, L0_xattn_ln1_g, L0_xattn_ln1_b, L0_xattn_Wq1, L0_xattn_Wk1, L0_xattn_Wv1, L0_xattn_Wo1, L0_xattn_bo1, L0_xattn_ln2_g, L0_xattn_ln2_b, L0_xattn_Wq2, L0_xattn_Wk2, L0_xattn_Wv2, L0_xattn_Wo2, L0_xattn_bo2, L0_xattn_ln3_g, L0_xattn_ln3_b, L0_xattn_Wp, L0_xattn_bp, L0_xattn_Wf2, L0_xattn_bf2, L1_xattn_Wq, L1_xattn_bq, L1_xattn_Wk, L1_xattn_bk, L1_xattn_Wv, L1_xattn_bv, L1_xattn_Wo, L1_xattn_bo, L1_xattn_ln_g, L1_xattn_ln_b, L1_xattn_W1, L1_xattn_b1, L1_xattn_W2, L1_xattn_b2, L2_xattn_Wq, L2_xattn_Wk, L2_xattn_Wv, L2_xattn_Wo, L2_xattn_bo, L2_xattn_gamma, L2_xattn_beta, L3_xattn_Wq, L3_xattn_Wk, L3_xattn_Wv, L3_xattn_Wo, L3_xattn_bo):
    import jax
    import jax.numpy as jnp

    def _L0_xattn_ref(x, context, ln1_g, ln1_b, Wq1, Wk1, Wv1, Wo1, bo1, ln2_g, ln2_b, Wq2, Wk2, Wv2, Wo2, bo2, ln3_g, ln3_b, Wp, bp, Wf2, bf2):
        import jax, jax.numpy as jnp
        import numpy as np
        DIM = 128
        H = 16
        DH = 64
        CTX_DIM = 96
        INNER_FF = 4 * DIM
        SCALE = DH ** (-0.5)
        EPS = 1e-05

        def layer_norm(x, g, b):
            mu = jnp.mean(x, axis=-1, keepdims=True)
            var = jnp.var(x, axis=-1, keepdims=True)
            return (x - mu) * jax.lax.rsqrt(var + EPS) * g + b

        def attention(x, ctx, Wq, Wk, Wv, Wo, bo):
            b, n, _ = x.shape
            m = ctx.shape[1]
            q = (x @ Wq).reshape(b, n, H, DH)
            k = (ctx @ Wk).reshape(b, m, H, DH)
            v = (ctx @ Wv).reshape(b, m, H, DH)
            sim = jnp.einsum('bihd,bjhd->bhij', q, k) * SCALE
            attn = jax.nn.softmax(sim, axis=-1)
            out = jnp.einsum('bhij,bjhd->bihd', attn, v).reshape(b, n, H * DH)
            return out @ Wo + bo
        h = layer_norm(x, ln1_g, ln1_b)
        x = x + attention(h, h, Wq1, Wk1, Wv1, Wo1, bo1)
        h = layer_norm(x, ln2_g, ln2_b)
        x = x + attention(h, context, Wq2, Wk2, Wv2, Wo2, bo2)
        h = layer_norm(x, ln3_g, ln3_b)
        proj = h @ Wp + bp
        a, gate = jnp.split(proj, 2, axis=-1)
        ff = a * jax.nn.gelu(gate, approximate=False) @ Wf2 + bf2
        return x + ff

    def _L1_xattn_ref(x, xf, Wq, bq, Wk, bk, Wv, bv, Wo, bo, ln_g, ln_b, W1, b1, W2, b2):
        import jax, jax.numpy as jnp
        import numpy as np
        LATENT = 128
        TEXT = 96
        HEADS = 16
        HEAD_DIM = LATENT // HEADS
        SCALE = HEAD_DIM ** (-0.5)
        LN_EPS = 1e-05
        B, Tx, D = x.shape
        Txf = xf.shape[1]
        q = (x @ Wq + bq).reshape(B, Tx, HEADS, HEAD_DIM).transpose(0, 2, 1, 3)
        k = (xf @ Wk + bk).reshape(B, Txf, HEADS, HEAD_DIM).transpose(0, 2, 1, 3)
        v = (xf @ Wv + bv).reshape(B, Txf, HEADS, HEAD_DIM).transpose(0, 2, 1, 3)
        scores = jnp.einsum('bhqd,bhkd->bhqk', q * SCALE, k)
        probs = jax.nn.softmax(scores, axis=-1)
        attn = jnp.einsum('bhqk,bhkd->bhqd', probs, v)
        out = attn.transpose(0, 2, 1, 3).reshape(B, Tx, D)
        out = out @ Wo + bo
        mu = jnp.mean(out, axis=-1, keepdims=True)
        var = jnp.var(out, axis=-1, keepdims=True)
        h = (out - mu) * jax.lax.rsqrt(var + LN_EPS) * ln_g + ln_b
        h = jax.nn.gelu(h @ W1 + b1, approximate=False)
        ffn = h @ W2 + b2
        out = out + ffn
        return x + out

    def _L2_xattn_ref(x, context, Wq, Wk, Wv, Wo, bo, gamma, beta):
        import jax, jax.numpy as jnp
        import numpy as np
        D_Q, D_CTX, N_HEADS, HEAD_DIM = (128, 96, 16, 64)
        INNER = N_HEADS * HEAD_DIM
        EPS = 1e-05

        def _layernorm(x, gamma, beta):
            mu = jnp.mean(x, axis=-1, keepdims=True)
            var = jnp.var(x, axis=-1, keepdims=True)
            return (x - mu) * jax.lax.rsqrt(var + EPS) * gamma + beta
        scale = HEAD_DIM ** (-0.5)
        h = _layernorm(x, gamma, beta)
        B, NQ, _ = x.shape
        NC = context.shape[1]
        Q = (h @ Wq).reshape(B, NQ, N_HEADS, HEAD_DIM)
        K = (context @ Wk).reshape(B, NC, N_HEADS, HEAD_DIM)
        V = (context @ Wv).reshape(B, NC, N_HEADS, HEAD_DIM)
        attn = jnp.einsum('bihd,bjhd->bhij', Q, K)
        attn = jax.nn.softmax(attn, axis=-1) * scale
        vals = jnp.einsum('bhij,bjhd->bihd', attn, V).reshape(B, NQ, INNER)
        out = vals @ Wo + bo
        return x + out

    def _L3_xattn_ref(x, context, Wq, Wk, Wv, Wo, bo):
        import jax, jax.numpy as jnp
        import numpy as np
        DIM = 128
        CTX_DIM = 96
        HEADS = 16
        HEAD_DIM = DIM // HEADS
        B, L, D = x.shape
        scale = HEAD_DIM ** (-0.5)
        q = jnp.einsum('bld,ed->ble', x, Wq)
        k = jnp.einsum('bcd,ed->bce', context, Wk)
        v = jnp.einsum('bcd,ed->bce', context, Wv)
        q = q.reshape(B, L, HEADS, HEAD_DIM).transpose(0, 2, 1, 3)
        k = k.reshape(B, -1, HEADS, HEAD_DIM).transpose(0, 2, 1, 3)
        v = v.reshape(B, -1, HEADS, HEAD_DIM).transpose(0, 2, 1, 3)
        attn = jnp.einsum('bhqd,bhkd->bhqk', q, k) * scale
        attn = jax.nn.softmax(attn, axis=-1)
        out = jnp.einsum('bhqk,bhkd->bhqd', attn, v)
        out = out.transpose(0, 2, 1, 3).reshape(B, L, D)
        return jnp.einsum('bld,ed->ble', out, Wo) + bo + x
    x = _L0_xattn_ref(x, ctx_768, L0_xattn_ln1_g, L0_xattn_ln1_b, L0_xattn_Wq1, L0_xattn_Wk1, L0_xattn_Wv1, L0_xattn_Wo1, L0_xattn_bo1, L0_xattn_ln2_g, L0_xattn_ln2_b, L0_xattn_Wq2, L0_xattn_Wk2, L0_xattn_Wv2, L0_xattn_Wo2, L0_xattn_bo2, L0_xattn_ln3_g, L0_xattn_ln3_b, L0_xattn_Wp, L0_xattn_bp, L0_xattn_Wf2, L0_xattn_bf2)
    x = _L1_xattn_ref(x, ctx_768, L1_xattn_Wq, L1_xattn_bq, L1_xattn_Wk, L1_xattn_bk, L1_xattn_Wv, L1_xattn_bv, L1_xattn_Wo, L1_xattn_bo, L1_xattn_ln_g, L1_xattn_ln_b, L1_xattn_W1, L1_xattn_b1, L1_xattn_W2, L1_xattn_b2)
    x = _L2_xattn_ref(x, ctx_768, L2_xattn_Wq, L2_xattn_Wk, L2_xattn_Wv, L2_xattn_Wo, L2_xattn_bo, L2_xattn_gamma, L2_xattn_beta)
    x = _L3_xattn_ref(x, ctx_768, L3_xattn_Wq, L3_xattn_Wk, L3_xattn_Wv, L3_xattn_Wo, L3_xattn_bo)
    return x

_drawn_inputs = setup_inputs


def setup_inputs(seed=0):
    import zlib

    import numpy as np

    out = dict(_drawn_inputs(seed))
    spreads = {'L0_xattn_ln1_g': (1.0, 0.6),
     'L0_xattn_ln1_b': (0.0, 0.634),
     'L0_xattn_bo1': (0.0, 0.1),
     'L0_xattn_ln2_g': (1.0, 0.6),
     'L0_xattn_ln2_b': (0.0, 2.0),
     'L0_xattn_bo2': (0.0, 0.1),
     'L0_xattn_ln3_g': (1.0, 0.6),
     'L0_xattn_ln3_b': (0.0, 0.8),
     'L0_xattn_bp': (0.0, 0.8),
     'L0_xattn_bf2': (0.0, 0.352),
     'L1_xattn_ln_g': (1.0, 0.6),
     'L1_xattn_ln_b': (0.0, 1.511),
     'L2_xattn_bo': (0.0, 0.332),
     'L2_xattn_gamma': (1.0, 0.6),
     'L2_xattn_beta': (0.0, 1.691)}
    factors = {'L0_xattn_Wq1': 8.0,
     'L0_xattn_Wk1': 8.0,
     'L0_xattn_Wv1': 3.259,
     'L0_xattn_Wo1': 3.472,
     'L0_xattn_Wq2': 8.0,
     'L0_xattn_Wk2': 8.0,
     'L0_xattn_Wp': 3.815,
     'L0_xattn_Wf2': 3.79,
     'L1_xattn_bq': 64.0,
     'L1_xattn_bk': 64.0,
     'L1_xattn_b1': 13.566,
     'L3_xattn_bo': 24.777,
     'L1_xattn_bv': 5.167,
     'L1_xattn_bo': 3.308,
     'L1_xattn_b2': 8.0}
    for name, (base, spread) in spreads.items():
        noise = np.random.default_rng([zlib.crc32(name.encode()), seed]).standard_normal(out[name].shape)
        drawn = base * np.exp(spread * noise) if base else spread * noise
        out[name] = jnp.asarray(drawn.astype(out[name].dtype))
    for name, factor in factors.items():
        out[name] = (out[name] * factor).astype(out[name].dtype)
    return out
```

```python
from contextlib import ExitStack

import concourse.bass as bass
from concourse import mybir

FP32 = mybir.dt.float32
ALU = mybir.AluOpType
ACT = mybir.ActivationFunctionType
AX = mybir.AxisListType

BATCHES, TOKENS, DIM = 32, 128, 128
CTX = 96
HEADS = 16
WIDE = 64
NARROW = DIM // HEADS
INNER = HEADS * WIDE
EPS = 1e-5
FF_HIDDEN = 4 * DIM
BANK = 512
SLOT_HEADS = 8
LANE = 32


class At:

    def __init__(self, n, i=None):
        self.n, self.i = n, i

    def plus(self, k):
        return At(self.n + k, self.i)

    def times(self, per, k=0):
        if self.i is None:
            return per * self.n + k
        return self.i * per + (per * self.n + k)

    @property
    def index(self):
        return self.times(1)


class Ring:

    BANKS = 4

    def __init__(self, order, steps, batches):
        self.batches = batches
        self.nth, self.fill, self.at_fill = {}, {}, []
        seen = {"act": 0, "dve": 0}
        self.per_step = dict.fromkeys(seen, 0)
        for _, _, engine in order:
            self.per_step[engine] += 1
        self.engine = {name: engine for name, _, engine in order}
        for step in steps:
            for name, lag, engine in order:
                if 0 <= step + lag < batches:
                    seen[engine] += 1
                    self.nth[name, step + lag] = seen[engine]
                    self.fill[name, step + lag] = len(self.at_fill)
                    self.at_fill.append((engine, seen[engine]))

    def count(self, name, at):
        base = self.nth[name, at.n]
        return base if at.i is None else at.i * self.per_step[self.engine[name]] + base

    def bank(self, name, at):
        return self.fill[name, at.n] % self.BANKS

    def before(self, name, at):
        n = self.fill[name, at.n] - self.BANKS
        if n < 0:
            return None
        engine, base = self.at_fill[n]
        return engine, (base if at.i is None else at.i * self.per_step[engine] + base)


def pipeline(engine, step, first, last, steady_first, steady_last):
    count = (steady_last - steady_first + 1) // 2 * 2
    for t in range(first, steady_first):
        step(At(t))
    with engine.Fori(0, count // 2) as turn:
        i = turn * 2
        step(At(steady_first, i))
        step(At(steady_first + 1, i))
    for t in range(steady_first + count, last + 1):
        step(At(t))


def build(nc, a, out):
    ctx = ExitStack()
    with ctx:
        def sb(name, shape):
            return ctx.enter_context(nc.sbuf_tensor(name, shape, FP32))

        def sem(name):
            return ctx.enter_context(nc.semaphore(name))

        x = sb("x", [TOKENS, BATCHES, DIM])
        ctxT = sb("ctxT", [CTX + 1, BATCHES, TOKENS])
        ident = sb("ident", [128, 128])
        ones_row = CTX
        W = {}
        for layer in ("L0a", "L0b", "L2"):
            for w in ("q", "k", "v"):
                W[layer, w] = sb(f"{layer}_w{w}", [DIM, INNER])
            W[layer, "o"] = sb(f"{layer}_wo", [128, INNER // 128, DIM])
        for layer in ("L1", "L3"):
            for w in ("q", "k", "v", "o"):
                W[layer, w] = sb(f"{layer}_w{w}", [128, DIM])
            for w in ("q", "k"):
                W[layer, w + "pad"] = sb(f"{layer}_w{w}pad", [128, 4, 4, LANE])
        for w in ("v", "o"):
            W["L3", w + "T"] = sb(f"L3_w{w}T", [128, DIM])
        bq_pad = sb("bq_pad", [128, 4])
        wp = sb("wp", [DIM, 2 * FF_HIDDEN])
        wf2 = sb("wf2", [128, 4, DIM])
        w1 = sb("w1", [DIM, FF_HIDDEN])
        w2 = sb("w2", [128, 4, DIM])
        bp = sb("bp", [128, 8])
        b1 = sb("b1", [128, 4])
        norm = {n: (sb(f"{n}_g", [DIM, 1]), sb(f"{n}_b", [DIM, 1])) for n in ("ln1", "ln2", "ln3", "L1_ln", "L2_ln")}
        bias = {n: sb(f"bias_{n}", [128, DIM]) for n in ("L0a", "L0b", "L0ff", "L1", "L1ff", "L2", "L3")}
        minus_half = sb("minus_half", [128, 1])
        eps = sb("eps", [128, 1])

        loaded = {g: sem(f"loaded_{g}") for g in ("x0", "x1", "ctx", "L0a", "L0b", "L0ff", "L1", "L1ff", "L2", "L3")}
        stored = sem("stored")
        loads = dict.fromkeys(loaded, 0)

        def load(queue, group, dst, src):
            loads[group] += 16
            queue.dma_start(dst, src).then_inc(loaded[group], 16)

        def column(v):
            return v.rearrange("(p a) -> p a", a=1)

        half = BATCHES // 2
        x_dram = a["x"].rearrange("b p d -> p b d")
        out_dram = out.rearrange("b p d -> p b d")

        def load_wide(queue, layer, q, k, v, o, bo, g, b, dkv):
            load(queue, layer, W[layer, "q"][:, :], q)
            load(queue, layer, W[layer, "k"][0:dkv, :], k)
            load(queue, layer, norm[g][0][:, :], column(a[b[0]]))
            load(queue, layer, norm[g][1][:, :], column(a[b[1]]))
            load(queue, layer, W[layer, "v"][0:dkv, :], v)
            load(queue, layer, W[layer, "o"][:, :, :], o.rearrange("(c p) n -> p c n", p=128))
            load(queue, layer, bias[layer][:, :], bo.partition_broadcast(128))

        with ExitStack() as work, nc.allow_non_contiguous_dma(reason="a few hundred bias elements, once"):
            ctx_rows = work.enter_context(nc.sbuf_tensor("ctx_rows", [TOKENS, BATCHES, CTX], FP32))
            banks = work.enter_context(nc.psum_tensor("setup_banks", [128, 8, BANK], FP32))
            ident_zero = sem("ident_zero")
            ident_ready = sem("ident_ready")
            padded_zero = sem("padded_zero")
            consts_ready = sem("consts_ready")
            ctx_bank_full = sem("ctx_bank_full")
            ctx_bank_copied = sem("ctx_bank_copied")
            w3_bank_full = sem("w3_bank_full")
            w3_copied = sem("w3_copied")
            w1_padded = sem("w1_padded")
            block = work.enter_context(nc.Block())

            @block.sync
            def _(sp):
                load(sp, "x0", x[:, 0:half, :], x_dram[:, 0:half, :])
                load(sp, "ctx", ctx_rows[:, :, :], a["ctx_768"].rearrange("b p d -> p b d"))
                load(sp, "x1", x[:, half:, :], x_dram[:, half:, :])
                load_wide(sp, "L0b", a["L0_xattn_Wq2"], a["L0_xattn_Wk2"], a["L0_xattn_Wv2"], a["L0_xattn_Wo2"],
                          a["L0_xattn_bo2"], "ln2", ("L0_xattn_ln2_g", "L0_xattn_ln2_b"), CTX)
                load(sp, "L0ff", wp[:, :], a["L0_xattn_Wp"])
                load(sp, "L0ff", wf2[:, :, :], a["L0_xattn_Wf2"].rearrange("(c p) n -> p c n", p=128))
                load(sp, "L0ff", bp[:, :], a["L0_xattn_bp"].rearrange("(c p) -> p c", p=128))
                load(sp, "L0ff", bias["L0ff"][:, :], a["L0_xattn_bf2"].partition_broadcast(128))
                load(sp, "L0ff", norm["ln3"][0][:, :], column(a["L0_xattn_ln3_g"]))
                load(sp, "L0ff", norm["ln3"][1][:, :], column(a["L0_xattn_ln3_b"]))
                load_wide(sp, "L2", a["L2_xattn_Wq"], a["L2_xattn_Wk"], a["L2_xattn_Wv"], a["L2_xattn_Wo"],
                          a["L2_xattn_bo"], "L2_ln", ("L2_xattn_gamma", "L2_xattn_beta"), CTX)

            @block.scalar
            def _(act):
                for w in ("q", "k", "v", "o"):
                    src = a[f"L3_xattn_W{w}"]
                    load(act, "L3", W["L3", w][:, 0:src.shape[1]], src)
                load(act, "L3", bias["L3"][:, :], a["L3_xattn_bo"].partition_broadcast(128))
                load(act, "L1", W["L1", "q"][:, :], a["L1_xattn_Wq"])
                for w in ("k", "v"):
                    load(act, "L1", W["L1", w][0:CTX, :], a[f"L1_xattn_W{w}"])
                    load(act, "L1", W["L1", w][ones_row:ones_row + 1, :],
                         a[f"L1_xattn_b{w}"].rearrange("(a n) -> a n", a=1))
                load(act, "L1", W["L1", "o"][:, :], a["L1_xattn_Wo"])
                load(act, "L1", bias["L1"][:, :], a["L1_xattn_bo"].partition_broadcast(128))
                act.wait_ge(padded_zero, 1)
                for j in range(4):
                    load(act, "L1", bq_pad[LANE * j:LANE * j + NARROW, :],
                         a["L1_xattn_bq"].rearrange("(g j d) -> j d g", j=4, d=NARROW)[j])
                load_wide(act, "L0a", a["L0_xattn_Wq1"], a["L0_xattn_Wk1"], a["L0_xattn_Wv1"], a["L0_xattn_Wo1"],
                          a["L0_xattn_bo1"], "ln1", ("L0_xattn_ln1_g", "L0_xattn_ln1_b"), DIM)
                load(act, "L1ff", w1[:, :], a["L1_xattn_W1"])
                load(act, "L1ff", w2[:, :, :], a["L1_xattn_W2"].rearrange("(c p) n -> p c n", p=128))
                load(act, "L1ff", b1[:, :], a["L1_xattn_b1"].rearrange("(c p) -> p c", p=128))
                load(act, "L1ff", bias["L1ff"][:, :], a["L1_xattn_b2"].partition_broadcast(128))
                load(act, "L1ff", norm["L1_ln"][0][:, :], column(a["L1_xattn_ln_g"]))
                load(act, "L1ff", norm["L1_ln"][1][:, :], column(a["L1_xattn_ln_b"]))

            @block.gpsimd
            def _(pool):
                nc.gpsimd.memset(ident[:, :], 0.0).then_inc(ident_zero, 1)
                pool.wait_ge(ident_zero, 1)
                nc.gpsimd.affine_select(out=ident[:, :], in_=ident[:, :], compare_op=ALU.not_equal, fill=1.0,
                                        base=0, pattern=[[-1, 128]], channel_multiplier=1).then_inc(ident_ready, 1)
                pool.wait_ge(ident_ready, 1)
                nc.gpsimd.memset(ctxT[ones_row:ones_row + 1, :, :], 1.0).then_inc(consts_ready, 1)
                pool.wait_ge(consts_ready, 1)
                nc.gpsimd.memset(minus_half[:, :], -0.5).then_inc(consts_ready, 1)
                nc.gpsimd.memset(eps[:, :], EPS).then_inc(consts_ready, 1)
                pool.wait_ge(consts_ready, 3)
                pool.wait_ge(padded_zero, 5)
                pool.wait_ge(loaded["L1"], 16 * 11)
                for n, (w, rows) in enumerate((("q", DIM), ("k", CTX + 1))):
                    if n:
                        pool.wait_ge(w1_padded, n)
                    nc.gpsimd.tensor_copy(W["L1", w + "pad"][0:rows, :, :, 0:NARROW],
                                          W["L1", w][0:rows, :].rearrange("p (g j d) -> p g j d", j=4, d=NARROW)
                                          ).then_inc(w1_padded, 1)
                pool.wait_ge(w1_padded, 2)

            @block.vector
            def _(dve):
                nc.vector.memset(bq_pad[:, :], 0.0).then_inc(padded_zero, 1)
                for layer in ("L1", "L3"):
                    for w in ("qpad", "kpad"):
                        nc.vector.memset(W[layer, w][:, :, :, :], 0.0).then_inc(padded_zero, 1)
                dve.wait_ge(padded_zero, 5)
                for n, (w, rows) in enumerate((("q", DIM), ("k", CTX), ("v", CTX), ("o", DIM))):
                    dve.wait_ge(w3_bank_full, n + 1)
                    src = banks[0:rows, n, 0:DIM]
                    if w in "qk":
                        nc.vector.tensor_copy(W["L3", w + "pad"][0:rows, :, :, 0:NARROW],
                                              src.rearrange("p (g j d) -> p g j d", j=4, d=NARROW)
                                              ).then_inc(w3_copied, 1)
                    else:
                        nc.vector.tensor_copy(W["L3", w + "T"][0:rows, :], src).then_inc(w3_copied, 1)
                for n in range(BATCHES // 4):
                    dve.wait_ge(ctx_bank_full, n + 1)
                    nc.vector.tensor_copy(ctxT[0:CTX, 4 * n:4 * n + 4, :],
                                          banks[0:CTX, 4 + n % 4, :].rearrange("p (b t) -> p b t", b=4)
                                          ).then_inc(ctx_bank_copied, 1)
                dve.wait_ge(ctx_bank_copied, BATCHES // 4)

            @block.tensor
            def _(pe):
                pe.wait_ge(ident_ready, 1)
                pe.wait_ge(loaded["L3"], 16 * 5)
                for n, (w, cols) in enumerate((("q", DIM), ("k", CTX), ("v", CTX), ("o", DIM))):
                    nc.tensor.transpose(banks[0:cols, n, 0:DIM], W["L3", w][:, 0:cols],
                                        ident[:, :]).then_inc(w3_bank_full, 1)
                pe.wait_ge(loaded["ctx"], 16)
                for n in range(BATCHES // 4):
                    if n >= 4:
                        pe.wait_ge(ctx_bank_copied, n - 3)
                    for k in range(4):
                        last = nc.tensor.transpose(banks[0:CTX, 4 + n % 4, 128 * k:128 * k + 128],
                                                   ctx_rows[:, 4 * n + k, :], ident[:, :])
                    last.then_inc(ctx_bank_full, 1)

        attention(nc, "L0a", x, x, None, W["L0a", "q"], W["L0a", "k"], W["L0a", "v"], W["L0a", "o"],
                  ident, minus_half, eps, bias["L0a"], norm["ln1"], head=WIDE, kv_rows=DIM, scale=WIDE ** -0.5,
                  waits=[(loaded["x0"], 16), (loaded["x1"], 16), (loaded["L0a"], loads["L0a"])])
        attention(nc, "L0b", x, x, ctxT, W["L0b", "q"], W["L0b", "k"], W["L0b", "v"], W["L0b", "o"],
                  ident, minus_half, eps, bias["L0b"], norm["ln2"], head=WIDE, kv_rows=CTX, scale=WIDE ** -0.5,
                  waits=[(loaded["L0b"], loads["L0b"])])
        feed_forward(nc, "L0ff", x, x, wp, wf2, bp, bias["L0ff"], norm["ln3"], ident, minus_half, eps, gated=True,
                     waits=[(loaded["L0ff"], loads["L0ff"])])
        with nc.sbuf_tensor("y", [TOKENS, BATCHES, DIM], FP32) as y:
            attention(nc, "L1", x, y, ctxT, W["L1", "qpad"], W["L1", "kpad"], W["L1", "v"], W["L1", "o"],
                      ident, minus_half, eps, bias["L1"], None, head=NARROW, kv_rows=CTX + 1, scale=NARROW ** -0.5,
                      waits=[(loaded["L1"], loads["L1"])], q_bias=bq_pad)
            feed_forward(nc, "L1ff", x, y, w1, w2, b1, bias["L1ff"], norm["L1_ln"], ident, minus_half, eps, gated=False,
                         waits=[(loaded["L1ff"], loads["L1ff"])])
        attention(nc, "L2", x, x, ctxT, W["L2", "q"], W["L2", "k"], W["L2", "v"], W["L2", "o"],
                  ident, minus_half, eps, bias["L2"], norm["L2_ln"], head=WIDE, kv_rows=CTX, scale=1.0,
                  v_ones=WIDE ** 0.5, waits=[(loaded["L2"], loads["L2"])])
        attention(nc, "L3", x, x, ctxT, W["L3", "qpad"], W["L3", "kpad"], W["L3", "vT"], W["L3", "oT"],
                  ident, minus_half, eps, bias["L3"], None, head=NARROW, kv_rows=CTX, scale=NARROW ** -0.5,
                  waits=[(loaded["L3"], loads["L3"])], store=(out_dram, stored))


def attention(nc, layer, x, dst, ctxT, wq, wk, wv, wo, ident, minus_half, eps, bias_o, norm, *, head, kv_rows, scale,
              waits, q_bias=None, v_ones=1.0, store=None):
    wide = head == WIDE
    residual = dst is x
    self_attention = ctxT is None
    q_engine = "dve" if q_bias is not None else "act"
    if wide:
        order = [("Wo", -1, "dve"), ("T0", 0, "act"), ("T1", 0, "act"), ("q0", 2, "act"), ("k0", 2, "act"),
                 ("PV0", 0, "dve"), ("PV1", 0, "dve"), ("T2", 0, "act"), ("T3", 0, "act"), ("q1", 2, "act"),
                 ("k1", 2, "act"), ("PV2", 0, "dve"), ("PV3", 0, "dve"), ("v0", 1, "act"), ("v1", 1, "act"),
                 ("hT", 3, "dve"), ("OT0", 0, "act"), ("OT1", 0, "act")]
    else:
        order = [("Wo", -1, "dve"), ("T0", 0, "act"), ("T1", 0, "act"), ("q0", 2, q_engine), ("k0", 2, "act"),
                 ("PV0", 0, "dve"), ("T2", 0, "act"), ("T3", 0, "act"), ("PV1", 0, "dve"), ("v0", 1, "act"),
                 ("hT", 3, "dve"), ("OT0", 0, "act")]
    first, last = -4, BATCHES
    steady_first, steady_last = 3, BATCHES - 5
    ring = Ring(order, range(first, last + 1), BATCHES)
    chunks = INNER // 128 if wide else 4
    v_cols = HEADS * head
    last_v = "v1" if wide else "v0"
    last_q, last_k = ("q1", "k1") if wide else ("q0", "k0")
    last_pv = "PV3" if wide else "PV1"
    last_ot = "OT1" if wide else "OT0"
    last_T = "T3"
    rows = WIDE if wide else LANE
    GROUP = 4

    def here(at, lag):
        return 0 <= at.n + lag < BATCHES

    with ExitStack() as ctx:
        def sb(name, shape):
            return ctx.enter_context(nc.sbuf_tensor(f"{layer}_{name}", shape, FP32))

        def sem(name):
            return ctx.enter_context(nc.semaphore(f"{layer}_{name}"))

        rows_h = sb("rows_h", [TOKENS, DIM])
        hT = sb("hT", [DIM, 2, TOKENS])
        cT = None if self_attention else sb("cT", [kv_rows, 2, TOKENS])
        qT = sb("qT", [128, 2, chunks, TOKENS])
        kT = sb("kT", [128, 2, chunks, TOKENS])
        v = sb("v", [TOKENS, 2, HEADS, head + 1])
        probs = sb("probs", [TOKENS, 2, SLOT_HEADS, TOKENS])
        probsT = sb("probsT", [TOKENS, HEADS, TOKENS])
        o = sb("o", [TOKENS, HEADS * head])
        oT = sb("oT", [128, HEADS * head // 128, TOKENS])
        x_bias = sb("x_bias", [TOKENS, 2, DIM]) if residual else None
        stats = sb("stats", [TOKENS, 2, 6])
        wait_carrier = sb("wait_carrier", [TOKENS, 1])
        moments = sb("moments", [TOKENS, 2, 2])
        var_eps = sb("var_eps", [TOKENS, 2, 1])
        rstd = sb("rstd", [TOKENS, 2, 1])
        row_max = sb("row_max", [TOKENS, 2, SLOT_HEADS])
        inv_sum = sb("inv_sum", [TOKENS, 4, SLOT_HEADS])
        scores = ctx.enter_context(nc.psum_tensor(f"{layer}_scores", [TOKENS, 2, 2, GROUP, TOKENS], FP32))
        ring_banks = ctx.enter_context(nc.psum_tensor(f"{layer}_ring", [128, Ring.BANKS, BANK], FP32))

        filled = {"act": sem("ring_filled_act"), "dve": sem("ring_filled_dve")}
        emptied = {"act": sem("ring_emptied_act"), "dve": sem("ring_emptied_dve")}
        ones_ready = sem("ones_ready")
        stats_ready = sem("stats_ready")
        moments_ready = sem("moments_ready")
        var_ready = sem("var_ready")
        rstd_ready = sem("rstd_ready")
        rows_h_ready = sem("rows_h_ready")
        cT_ready = sem("cT_ready")
        x_bias_ready = sem("x_bias_ready")
        scores_full = sem("scores_full")
        max_ready = sem("max_ready")
        shifted = sem("shifted")
        probs_ready = sem("probs_ready")
        sums_inverted = sem("sums_inverted")
        block = ctx.enter_context(nc.Block())

        def bank(name, at):
            return ring_banks[:, ring.bank(name, at), :]

        def await_filled(engine, name, at):
            engine.wait_ge(filled[ring.engine[name]], ring.count(name, at))

        def await_emptied(engine, name, at):
            engine.wait_ge(emptied[ring.engine[name]], ring.count(name, at))

        def steps(engine, step):
            pipeline(engine, step, first, last, steady_first, steady_last)

        @block.tensor
        def _(pe):
            for semaphore, value in waits:
                pe.wait_ge(semaphore, value)

            def start_fill(name, at):
                before = ring.before(name, at)
                if before:
                    pe.wait_ge(emptied[before[0]], before[1])
                return bank(name, at)

            def filled_by(instruction, name):
                instruction.then_inc(filled[ring.engine[name]], 1)

            def score(at, s):
                await_emptied(pe, f"q{s}" if wide else "q0", at)
                await_emptied(pe, f"k{s}" if wide else "k0", at)
                if at.n >= 1:
                    pe.wait_ge(shifted, at.times(2, s - 1))
                p = at.n % 2
                for i in range(GROUP):
                    for r in range(2):
                        c, lane = (GROUP * s + i, r) if wide else (i, 2 * s + r)
                        part = slice(rows * lane, rows * lane + rows)
                        last = nc.tensor.matmul(scores[:, s, r, i, :], qT[part, p, c, :], kT[part, p, c, :],
                                                start=True, stop=True, tile_position=(rows * lane, 0))
                last.then_inc(scores_full, 1)

            def transpose_probs(at, n):
                s, r = divmod(n, 2)
                if r == 0:
                    pe.wait_ge(probs_ready, at.times(2, s + 1))
                to = start_fill(f"T{n}", at)
                for i in range(GROUP):
                    last = nc.tensor.transpose(to[:, TOKENS * i:TOKENS * (i + 1)], probs[:, s, GROUP * r + i, :],
                                               ident[:, :])
                filled_by(last, f"T{n}")

            def project_T(name, at, w, src, src_rows, c0):
                to = start_fill(name, at)
                for c in range(4):
                    last = nc.tensor.matmul(to[:, TOKENS * c:TOKENS * (c + 1)], w[0:src_rows, c0 + c],
                                            src, start=True, stop=True)
                filled_by(last, name)

            def queries(at, n):
                if n == 0:
                    await_emptied(pe, "hT", at)
                w = wq[:, :].rearrange("p (c n) -> p c n", n=128) if wide else wq[:, :, :, :].rearrange("p c j n -> p c (j n)")
                project_T(f"q{n}", at, w, hT[:, at.n % 2, :], DIM, 4 * n)

            def keys(at, n):
                if n == 0 and not self_attention:
                    pe.wait_ge(cT_ready, at.times(1, 1))
                w = wk[:, :].rearrange("p (c n) -> p c n", n=128) if wide else wk[:, :, :, :].rearrange("p c j n -> p c (j n)")
                src = hT if self_attention else cT
                project_T(f"k{n}", at, w, src[0:kv_rows, at.n % 2, :], kv_rows, 4 * n)

            def values(at, n):
                to = start_fill(f"v{n}", at)
                src = hT if self_attention else cT
                cols = min(BANK, v_cols)
                filled_by(nc.tensor.matmul(to[:, 0:cols], src[0:kv_rows, at.n % 2, :],
                                           wv[0:kv_rows, cols * n:cols * (n + 1)], start=True, stop=True), f"v{n}")

            def weigh(at, n):
                if n == 0:
                    await_emptied(pe, last_v, at)
                groups = [n] if wide else [2 * n, 2 * n + 1]
                for group in groups:
                    await_emptied(pe, f"T{group}", at)
                to = start_fill(f"PV{n}", at)
                for k, group in enumerate(groups):
                    s, r = divmod(group, 2)
                    for i in range(GROUP):
                        h = 2 * (GROUP * s + i) + r if wide else 4 * i + 2 * s + r
                        c = (GROUP * k + i) * (head + 1)
                        last = nc.tensor.matmul(to[:, c:c + head + 1], probsT[:, GROUP * group + i, :],
                                                v[:, at.n % 2, h, :], start=True, stop=True)
                filled_by(last, f"PV{n}")

            def transpose_h(at):
                pe.wait_ge(rows_h_ready, at.times(1, 1))
                filled_by(nc.tensor.transpose(start_fill("hT", at)[:, 0:TOKENS], rows_h[:, :], ident[:, :]), "hT")

            def transpose_o(at, n):
                if n == 0:
                    await_emptied(pe, last_pv, at)
                to = start_fill(f"OT{n}", at)
                for c in range(4 if wide else 1):
                    last = nc.tensor.transpose(to[:, TOKENS * c:TOKENS * (c + 1)],
                                               o[:, BANK * n + 128 * c:BANK * n + 128 * (c + 1)], ident[:, :])
                filled_by(last, f"OT{n}")

            def project_out(at):
                await_emptied(pe, last_ot, at)
                to = start_fill("Wo", at)
                pieces = HEADS * head // 128
                for c in range(pieces):
                    w = wo[:, c, :] if wide else wo[:, :]
                    last = nc.tensor.matmul(to[:, 0:DIM], oT[:, c, :], w, start=c == 0, stop=c == pieces - 1)
                filled_by(last, "Wo")

            def step(t):
                if here(t, 1):
                    score(t.plus(1), 0)
                if here(t, -1):
                    project_out(t.plus(-1))
                if here(t, 0):
                    transpose_probs(t, 0)
                    transpose_probs(t, 1)
                if here(t, 2):
                    queries(t.plus(2), 0)
                    keys(t.plus(2), 0)
                if here(t, 0):
                    weigh(t, 0)
                    if wide:
                        weigh(t, 1)
                if here(t, 1):
                    score(t.plus(1), 1)
                if here(t, 0):
                    transpose_probs(t, 2)
                    transpose_probs(t, 3)
                if wide and here(t, 2):
                    queries(t.plus(2), 1)
                    keys(t.plus(2), 1)
                if here(t, 0):
                    if wide:
                        weigh(t, 2)
                        weigh(t, 3)
                    else:
                        weigh(t, 1)
                if here(t, 1):
                    values(t.plus(1), 0)
                    if wide:
                        values(t.plus(1), 1)
                if here(t, 3):
                    transpose_h(t.plus(3))
                if here(t, 0):
                    transpose_o(t, 0)
                    if wide:
                        transpose_o(t, 1)

            steps(pe, step)

        @block.scalar
        def _(act):
            def empty(name, at, to, cols):
                await_filled(act, name, at)
                src = bank(name, at)[:, 0:cols]
                nc.scalar.activation(to, src, ACT.Copy).then_inc(emptied["act"], 1)

            def exponentiate(at, s):
                act.wait_ge(shifted, at.times(2, s + 1))
                nc.scalar.activation(probs[:, s, :, :], probs[:, s, :, :], ACT.Exp,
                                     scale=scale).then_inc(probs_ready, 1)

            def projections(at, n):
                p = at.n % 2
                if q_engine == "act":
                    empty(f"q{n}", at, qT[:, p, 4 * n:4 * n + 4, :].rearrange("p c t -> p (c t)"), BANK)
                empty(f"k{n}", at, kT[:, p, 4 * n:4 * n + 4, :].rearrange("p c t -> p (c t)"), BANK)

            def values(at, n):
                await_filled(act, f"v{n}", at)
                cols = min(BANK, v_cols)
                heads = cols // head
                if n == 0 and at.n < 2 and at.i is None:
                    act.wait_ge(ones_ready, 1)
                nc.scalar.activation(v[:, at.n % 2, heads * n:heads * (n + 1), 0:head],
                                     bank(f"v{n}", at)[:, 0:cols].rearrange("p (h d) -> p h d", d=head),
                                     ACT.Copy).then_inc(emptied["act"], 1)

            def turned_probs(at, n):
                empty(f"T{n}", at, probsT[:, GROUP * n:GROUP * (n + 1), :].rearrange("p h t -> p (h t)"), BANK)

            def step(t):
                if here(t, 0):
                    turned_probs(t, 0)
                    turned_probs(t, 1)
                if here(t, 2):
                    projections(t.plus(2), 0)
                if here(t, 1):
                    exponentiate(t.plus(1), 0)
                if here(t, 0):
                    turned_probs(t, 2)
                    turned_probs(t, 3)
                if wide and here(t, 2):
                    projections(t.plus(2), 1)
                if here(t, 1):
                    exponentiate(t.plus(1), 1)
                    values(t.plus(1), 0)
                    if wide:
                        values(t.plus(1), 1)
                if here(t, 0):
                    for n in range(2 if wide else 1):
                        pieces = 4 if wide else 1
                        empty(f"OT{n}", t, oT[:, pieces * n:pieces * (n + 1), :].rearrange("p c t -> p (c t)"),
                              TOKENS * pieces)

            steps(act, step)

        @block.vector
        def _(dve):
            nc.vector.memset(v[:, :, :, head:head + 1], v_ones).then_inc(ones_ready, 1)
            for semaphore, value in waits:
                dve.wait_ge(semaphore, value)

            def statistics(at):
                p = at.n % 2
                nc.vector.bn_stats(stats[:, p, :], x[:, at.index, :]).then_inc(stats_ready, 1)
                dve.wait_ge(stats_ready, at.times(1, 1))
                nc.vector.memset(wait_carrier[:, :], 0.0)
                nc.vector.bn_aggr(moments[:, p, :], stats[:, p, :]).then_inc(moments_ready, 1)

            def normalise(at):
                p = at.n % 2
                dve.wait_ge(moments_ready, at.times(1, 1))
                dve.wait_ge(rstd_ready, at.times(1, 1))
                if at.n >= 1:
                    await_filled(dve, "hT", at.plus(-1))
                nc.vector.tensor_scalar(rows_h[:, :], x[:, at.index, :], moments[:, p, 0:1], rstd[:, p, :],
                                        ALU.subtract, ALU.mult).then_inc(rows_h_ready, 1)

            def row_maxima(at, s):
                dve.wait_ge(scores_full, at.times(2, s + 1))
                nc.vector.tensor_reduce(row_max[:, s, :], scores[:, s, :, :, :].rearrange("p r i k -> p (r i) k"),
                                        AX.X, ALU.max).then_inc(max_ready, 1)

            def subtract_maxima(at, s):
                dve.wait_ge(max_ready, at.times(2, s + 1))
                if at.n >= 1:
                    await_filled(dve, f"T{2 * s + 1}", at.plus(-1))
                nc.vector.tensor_tensor(probs[:, s, :, :], scores[:, s, :, :, :].rearrange("p r i k -> p (r i) k"),
                                        row_max[:, s, :].unsqueeze(2).to_broadcast([TOKENS, SLOT_HEADS, TOKENS]),
                                        ALU.subtract).then_inc(shifted, 1)

            def divide(at, n):
                await_filled(dve, f"PV{n}", at)
                heads = GROUP if wide else 2 * GROUP
                pv = bank(f"PV{n}", at)[:, 0:heads * (head + 1)].rearrange("p (h d) -> p h d", d=head + 1)
                groups = 4 if wide else 2
                nc.vector.reciprocal(inv_sum[:, n, 0:heads], pv[:, :, head]).then_inc(sums_inverted, 1)
                dve.wait_ge(sums_inverted, at.times(groups, n + 1))
                if wide:
                    s, r = divmod(n, 2)
                    to = o[:, :].rearrange("p (s i r d) -> p s r i d", s=2, r=2, d=head)[:, s, r, :, :]
                    nc.vector.tensor_tensor(to, pv[:, :, 0:head],
                                            inv_sum[:, n, 0:heads].unsqueeze(2).to_broadcast([TOKENS, heads, head]),
                                            ALU.mult).then_inc(emptied["dve"], 1)
                else:
                    to = o[:, :].rearrange("p (i s r d) -> p s r i d", s=2, r=2, d=head)[:, n, :, :, :]
                    pv4 = pv.rearrange("p (r i) d -> p r i d", r=2)
                    inv4 = inv_sum[:, n, 0:heads].rearrange("p (r i) -> p r i", r=2)
                    nc.vector.tensor_tensor(to, pv4[:, :, :, 0:head],
                                            inv4.unsqueeze(3).to_broadcast([TOKENS, 2, GROUP, head]),
                                            ALU.mult).then_inc(emptied["dve"], 1)

            def turned_h(at):
                await_filled(dve, "hT", at)
                src = bank("hT", at)[:, 0:TOKENS]
                if norm is None:
                    nc.vector.tensor_copy(hT[:, at.n % 2, :], src).then_inc(emptied["dve"], 1)
                else:
                    nc.vector.tensor_scalar(hT[:, at.n % 2, :], src, norm[0][:, :], norm[1][:, :],
                                            ALU.mult, ALU.add).then_inc(emptied["dve"], 1)

            def biased_queries(at):
                await_filled(dve, "q0", at)
                nc.vector.tensor_tensor(qT[:, at.n % 2, :, :],
                                        bank("q0", at).rearrange("p (c t) -> p c t", t=TOKENS),
                                        q_bias[:, :].unsqueeze(2).to_broadcast([128, 4, TOKENS]),
                                        ALU.add).then_inc(emptied["dve"], 1)

            def finish(at):
                await_filled(dve, "Wo", at)
                if residual:
                    dve.wait_ge(x_bias_ready, at.times(1, 1))
                    plus = x_bias[:, at.n % 2, :]
                else:
                    plus = bias_o[:, :]
                nc.vector.tensor_tensor(dst[:, at.index, :], bank("Wo", at)[:, 0:DIM], plus,
                                        ALU.add).then_inc(emptied["dve"], 1)

            def step(t):
                if here(t, 1):
                    row_maxima(t.plus(1), 0)
                if here(t, -1):
                    finish(t.plus(-1))
                if here(t, 1):
                    subtract_maxima(t.plus(1), 0)
                if norm is not None and here(t, 4):
                    statistics(t.plus(4))
                if q_engine == "dve" and here(t, 2):
                    biased_queries(t.plus(2))
                if here(t, 0):
                    divide(t, 0)
                    if wide:
                        divide(t, 1)
                if norm is not None and here(t, 3):
                    normalise(t.plus(3))
                if here(t, 1):
                    row_maxima(t.plus(1), 1)
                    subtract_maxima(t.plus(1), 1)
                if here(t, 0):
                    if wide:
                        divide(t, 2)
                        divide(t, 3)
                    else:
                        divide(t, 1)
                if here(t, 3):
                    turned_h(t.plus(3))

            steps(dve, step)

        @block.gpsimd
        def _(pool):
            for semaphore, value in waits:
                pool.wait_ge(semaphore, value)

            def inverse_deviation(at):
                p = at.n % 2
                pool.wait_ge(moments_ready, at.times(1, 1))
                if at.n >= 2:
                    pool.wait_ge(rows_h_ready, at.times(1, -1))
                nc.gpsimd.tensor_tensor(var_eps[:, p, :], moments[:, p, 1:2], eps[:, :], ALU.add).then_inc(var_ready, 1)
                pool.wait_ge(var_ready, at.times(1, 1))
                nc.gpsimd.tensor_tensor(rstd[:, p, :], var_eps[:, p, :], minus_half[:, :],
                                        ALU.pow).then_inc(rstd_ready, 1)

            def copy_rows(at):
                if at.n >= 1:
                    await_filled(pool, "hT", at.plus(-1))
                nc.gpsimd.tensor_copy(rows_h[:, :], x[:, at.index, :]).then_inc(rows_h_ready, 1)

            def add_bias(at):
                if at.n >= 2:
                    await_emptied(pool, "Wo", at.plus(-2))
                nc.gpsimd.tensor_tensor(x_bias[:, at.n % 2, :], x[:, at.index, :], bias_o[:, :],
                                        ALU.add).then_inc(x_bias_ready, 1)

            def stage_context(at):
                if at.n >= 2:
                    await_filled(pool, last_v, at.plus(-2))
                nc.gpsimd.tensor_copy(cT[0:kv_rows, at.n % 2, :],
                                      ctxT[0:kv_rows, at.index, :]).then_inc(cT_ready, 1)

            def step(t):
                if norm is not None and here(t, 4):
                    inverse_deviation(t.plus(4))
                if norm is None and here(t, 3):
                    copy_rows(t.plus(3))
                if residual and here(t, 1):
                    add_bias(t.plus(1))
                if not self_attention and here(t, 3):
                    stage_context(t.plus(3))

            steps(pool, step)

        if store is not None:
            @block.sync
            def _(sp):
                out_dram, stored = store
                for b in range(BATCHES):
                    await_emptied(sp, "Wo", At(b))
                    sp.dma_start(out_dram[:, b, :], dst[:, b, :]).then_inc(stored, 16)
                sp.wait_ge(stored, 16 * BATCHES)


def feed_forward(nc, layer, x, src, w_in, w_out, b_in, bias_out, norm, ident, minus_half, eps, *, gated, waits):
    SIZE = 4
    GROUPS = BATCHES // SIZE
    CHUNKS = FF_HIDDEN // 128
    add_src = src is not x

    def here(at, lag):
        return 0 <= at.n + lag < GROUPS

    with ExitStack() as ctx:
        def sb(name, shape):
            return ctx.enter_context(nc.sbuf_tensor(f"{layer}_{name}", shape, FP32))

        def sem(name):
            return ctx.enter_context(nc.semaphore(f"{layer}_{name}"))

        stats = sb("stats", [TOKENS, SIZE, 6])
        wait_carrier = sb("wait_carrier", [TOKENS, 1])
        moments = sb("moments", [TOKENS, SIZE, 2])
        var_eps = sb("var_eps", [TOKENS, SIZE])
        rstd = sb("rstd", [TOKENS, SIZE])
        rows_h = sb("rows_h", [TOKENS, SIZE, DIM])
        hT = sb("hT", [DIM, 2, SIZE * TOKENS])
        gelu = sb("gelu", [128, 2, SIZE * TOKENS]) if gated else None
        hidden = sb("hidden", [128, 2, CHUNKS, SIZE * TOKENS])
        base = sb("base", [TOKENS, 2, SIZE, DIM])
        in_banks = ctx.enter_context(nc.psum_tensor(f"{layer}_in", [128, 4, BANK], FP32))
        out_banks = ctx.enter_context(nc.psum_tensor(f"{layer}_out", [128, 2, BANK], FP32))
        turn_banks = ctx.enter_context(nc.psum_tensor(f"{layer}_turn", [128, 2, BANK], FP32))

        stats_ready = sem("stats_ready")
        moments_ready = sem("moments_ready")
        var_ready = sem("var_ready")
        rstd_ready = sem("rstd_ready")
        rows_ready = sem("rows_ready")
        turned = sem("turned")
        hT_ready = sem("hT_ready")
        gate_full = sem("gate_full")
        value_full = sem("value_full")
        gelu_ready = sem("gelu_ready")
        hidden_ready = sem("hidden_ready")
        out_full = sem("out_full")
        out_added = sem("out_added")
        base_sum = sem("base_sum")
        base_ready = sem("base_ready")
        block = ctx.enter_context(nc.Block())

        def steps(engine, step):
            pipeline(engine, step, -2, GROUPS - 1, 2, GROUPS - 3)

        def gate_bank(c):
            return in_banks[:, c % 2 if gated else c, :]

        @block.tensor
        def _(pe):
            for semaphore, value in waits:
                pe.wait_ge(semaphore, value)

            def transpose_rows(at):
                pe.wait_ge(rows_ready, at.times(SIZE, SIZE))
                if at.n >= 2:
                    pe.wait_ge(hT_ready, at.times(1, -1))
                for k in range(SIZE):
                    last = nc.tensor.transpose(turn_banks[:, at.n % 2, 128 * k:128 * (k + 1)], rows_h[:, k, :],
                                               ident[:, :])
                last.then_inc(turned, 1)

            def expand(at):
                pe.wait_ge(hT_ready, at.times(1, 1))
                for c in range(CHUNKS):
                    if gated:
                        before = at.times(CHUNKS, c - 1)
                        if at.n > 0 or c >= 2:
                            pe.wait_ge(gelu_ready, before)
                    elif at.n > 0:
                        pe.wait_ge(hidden_ready, at.times(CHUNKS, c - 3))
                    gate_col = FF_HIDDEN + 128 * c if gated else 128 * c
                    nc.tensor.matmul(gate_bank(c), w_in[:, gate_col:gate_col + 128], hT[:, at.n % 2, :],
                                     start=True, stop=True).then_inc(gate_full, 1)
                    if gated:
                        if at.n > 0 or c >= 2:
                            pe.wait_ge(hidden_ready, before)
                        nc.tensor.matmul(in_banks[:, 2 + c % 2, :], w_in[:, 128 * c:128 * c + 128],
                                         hT[:, at.n % 2, :], start=True, stop=True).then_inc(value_full, 1)

            def contract(at):
                pe.wait_ge(hidden_ready, at.times(CHUNKS, CHUNKS))
                if at.n >= 2:
                    pe.wait_ge(out_added, at.times(1, -1))
                for k in range(SIZE):
                    for c in range(CHUNKS):
                        last = nc.tensor.matmul(out_banks[:, at.n % 2, 128 * k:128 * (k + 1)],
                                                hidden[:, at.n % 2, c, 128 * k:128 * (k + 1)], w_out[:, c, :],
                                                start=c == 0, stop=c == CHUNKS - 1)
                last.then_inc(out_full, 1)

            def step(t):
                if here(t, 1):
                    expand(t.plus(1))
                if here(t, 2):
                    transpose_rows(t.plus(2))
                if here(t, 0):
                    contract(t)

            steps(pe, step)

        @block.scalar
        def _(act):
            for semaphore, value in waits:
                act.wait_ge(semaphore, value)

            def activate(at):
                for c in range(CHUNKS):
                    act.wait_ge(gate_full, at.times(CHUNKS, c + 1))
                    if gated:
                        if at.n > 0 or c >= 2:
                            act.wait_ge(hidden_ready, at.times(CHUNKS, c - 1))
                        nc.scalar.activation(gelu[:, c % 2, :], gate_bank(c), ACT.Gelu,
                                             bias=b_in[:, CHUNKS + c:CHUNKS + c + 1]).then_inc(gelu_ready, 1)
                    else:
                        if at.n >= 2:
                            act.wait_ge(out_full, at.times(1, -1))
                        nc.scalar.activation(hidden[:, at.n % 2, c, :], gate_bank(c), ACT.Gelu,
                                             bias=b_in[:, c:c + 1]).then_inc(hidden_ready, 1)

            def step(t):
                if here(t, 1):
                    activate(t.plus(1))

            steps(act, step)

        @block.vector
        def _(dve):
            for semaphore, value in waits:
                dve.wait_ge(semaphore, value)

            def statistics(at):
                for k in range(SIZE):
                    if k == 0 and at.n >= 1:
                        dve.wait_ge(rstd_ready, at.times(1, 0))
                    nc.vector.bn_stats(stats[:, k, :], src[:, at.times(SIZE, k), :]).then_inc(stats_ready, 1)
                for k in range(SIZE):
                    if k == 0:
                        dve.wait_ge(stats_ready, at.times(SIZE, SIZE))
                        nc.vector.memset(wait_carrier[:, :], 0.0)
                    nc.vector.bn_aggr(moments[:, k, :], stats[:, k, :]).then_inc(moments_ready, 1)

            def normalise(at):
                dve.wait_ge(moments_ready, at.times(SIZE, SIZE))
                dve.wait_ge(rstd_ready, at.times(1, 1))
                if at.n >= 1:
                    dve.wait_ge(turned, at.times(1, 0))
                for k in range(SIZE):
                    nc.vector.tensor_scalar(rows_h[:, k, :], src[:, at.times(SIZE, k), :], moments[:, k, 0:1],
                                            rstd[:, k:k + 1], ALU.subtract, ALU.mult).then_inc(rows_ready, 1)

            def scale_turned(at):
                dve.wait_ge(turned, at.times(1, 1))
                nc.vector.tensor_scalar(hT[:, at.n % 2, :], turn_banks[:, at.n % 2, :], norm[0][:, :], norm[1][:, :],
                                        ALU.mult, ALU.add).then_inc(hT_ready, 1)

            def gate(at):
                for c in range(CHUNKS):
                    dve.wait_ge(value_full, at.times(CHUNKS, c + 1))
                    dve.wait_ge(gelu_ready, at.times(CHUNKS, c + 1))
                    nc.vector.scalar_tensor_tensor(hidden[:, at.n % 2, c, :], in_banks[:, 2 + c % 2, :],
                                                   b_in[:, c:c + 1], gelu[:, c % 2, :], ALU.add,
                                                   ALU.mult).then_inc(hidden_ready, 1)

            def finish(at):
                dve.wait_ge(out_full, at.times(1, 1))
                dve.wait_ge(base_ready, at.times(SIZE, SIZE))
                nc.vector.tensor_tensor(x[:, bass.ds(at.times(SIZE), SIZE), :],
                                        out_banks[:, at.n % 2, :].rearrange("p (k d) -> p k d", k=SIZE),
                                        base[:, at.n % 2, :, :], ALU.add).then_inc(out_added, 1)

            def step(t):
                if here(t, 2):
                    statistics(t.plus(2))
                if gated and here(t, 1):
                    gate(t.plus(1))
                if here(t, 2):
                    normalise(t.plus(2))
                    scale_turned(t.plus(2))
                if here(t, 0):
                    finish(t)

            steps(dve, step)

        @block.gpsimd
        def _(pool):
            for semaphore, value in waits:
                pool.wait_ge(semaphore, value)

            def inverse_deviation(at):
                pool.wait_ge(moments_ready, at.times(SIZE, SIZE))
                if at.n >= 1:
                    pool.wait_ge(rows_ready, at.times(SIZE, 0))
                nc.gpsimd.tensor_tensor(var_eps[:, :], moments[:, :, 1], eps[:, :].to_broadcast([TOKENS, SIZE]),
                                        ALU.add).then_inc(var_ready, 1)
                pool.wait_ge(var_ready, at.times(1, 1))
                nc.gpsimd.tensor_tensor(rstd[:, :], var_eps[:, :], minus_half[:, :].to_broadcast([TOKENS, SIZE]),
                                        ALU.pow).then_inc(rstd_ready, 1)

            def residual(at):
                if at.n >= 2:
                    pool.wait_ge(out_added, at.times(1, -1))
                for k in range(SIZE):
                    row = base[:, at.n % 2, k, :]
                    if add_src:
                        nc.gpsimd.tensor_tensor(row, x[:, at.times(SIZE, k), :], src[:, at.times(SIZE, k), :],
                                                ALU.add).then_inc(base_sum, 1)
                        pool.wait_ge(base_sum, at.times(SIZE, k + 1))
                        nc.gpsimd.tensor_tensor(row, row, bias_out[:, :], ALU.add).then_inc(base_ready, 1)
                    else:
                        nc.gpsimd.tensor_tensor(row, x[:, at.times(SIZE, k), :], bias_out[:, :],
                                                ALU.add).then_inc(base_ready, 1)

            def step(t):
                if here(t, 2):
                    inverse_deviation(t.plus(2))
                if here(t, 1):
                    residual(t.plus(1))

            steps(pool, step)


def kernel(**inputs):
    import numpy as _np
    import concourse.bacc as _bacc
    from concourse import mybir as _mybir
    from concourse.bass_utils import run_bass_kernel_spmd as _run

    nc = _bacc.Bacc("TRN2", target_bir_lowering=False, num_devices=1)
    arrays, aps = {}, {}
    for name in inputs:
        value = _np.ascontiguousarray(inputs[name])
        arrays[f"in_{name}"] = value
        aps[name] = nc.dram_tensor(f"in_{name}", value.shape, _mybir.dt.from_np(value.dtype),
                                   kind="ExternalInput").ap()
    result = nc.dram_tensor("out_x", (BATCHES, TOKENS, DIM), _mybir.dt.float32, kind="ExternalOutput").ap()
    build(nc, aps, result)
    done = _run(nc, [arrays], core_ids=[0])
    return done.results[0]["out_x"]
```

```python
from contextlib import ExitStack

import concourse.bass as bass
from concourse import mybir

FP32 = mybir.dt.float32
ALU = mybir.AluOpType
ACT = mybir.ActivationFunctionType
AX = mybir.AxisListType

BATCHES, TOKENS, DIM = 32, 128, 128
CTX = 96
HEADS = 16
WIDE = 64
NARROW = DIM // HEADS
INNER = HEADS * WIDE
EPS = 1e-5
FF_HIDDEN = 4 * DIM
BANK = 512
SLOT_HEADS = 8


class At:

    def __init__(self, n, i=None):
        self.n, self.i = n, i

    def plus(self, k):
        return At(self.n + k, self.i)

    def times(self, per, k=0):
        if self.i is None:
            return per * self.n + k
        return self.i * per + (per * self.n + k)

    @property
    def index(self):
        return self.times(1)


class Ring:

    BANKS = 4

    def __init__(self, order, steps, batches):
        self.batches = batches
        self.nth, self.fill, self.at_fill = {}, {}, []
        seen = {"act": 0, "dve": 0}
        self.per_step = dict.fromkeys(seen, 0)
        for _, _, engine in order:
            self.per_step[engine] += 1
        self.engine = {name: engine for name, _, engine in order}
        for step in steps:
            for name, lag, engine in order:
                if 0 <= step + lag < batches:
                    seen[engine] += 1
                    self.nth[name, step + lag] = seen[engine]
                    self.fill[name, step + lag] = len(self.at_fill)
                    self.at_fill.append((engine, seen[engine]))

    def count(self, name, at):
        base = self.nth[name, at.n]
        return base if at.i is None else at.i * self.per_step[self.engine[name]] + base

    def bank(self, name, at):
        return self.fill[name, at.n] % self.BANKS

    def before(self, name, at):
        n = self.fill[name, at.n] - self.BANKS
        if n < 0:
            return None
        engine, base = self.at_fill[n]
        return engine, (base if at.i is None else at.i * self.per_step[engine] + base)


def pipeline(engine, step, first, last, steady_first, steady_last):
    count = (steady_last - steady_first + 1) // 2 * 2
    for t in range(first, steady_first):
        step(At(t))
    with engine.Fori(0, count // 2) as turn:
        i = turn * 2
        step(At(steady_first, i))
        step(At(steady_first + 1, i))
    for t in range(steady_first + count, last + 1):
        step(At(t))


def build(nc, a, out):
    ctx = ExitStack()
    with ctx:
        def sb(name, shape):
            return ctx.enter_context(nc.sbuf_tensor(name, shape, FP32))

        def sem(name):
            return ctx.enter_context(nc.semaphore(name))

        x = sb("x", [TOKENS, BATCHES, DIM])
        ctxT = sb("ctxT", [CTX + 1, BATCHES, TOKENS])
        ident = sb("ident", [128, 128])
        ones_row = CTX
        W = {}
        for layer in ("L0a", "L0b", "L2"):
            for w in ("q", "k", "v"):
                W[layer, w] = sb(f"{layer}_w{w}", [DIM, INNER])
            W[layer, "o"] = sb(f"{layer}_wo", [128, INNER // 128, DIM])
        for layer in ("L1", "L3"):
            for w in ("q", "k", "v", "o"):
                W[layer, w] = sb(f"{layer}_w{w}", [128, DIM])
        for w in ("q", "k", "v", "o"):
            W["L3", w + "T"] = sb(f"L3_w{w}T", [128, DIM])
        bq = sb("bq", [128, 1])
        head_mask = sb("head_mask", [128, SLOT_HEADS])
        wp = sb("wp", [DIM, 2 * FF_HIDDEN])
        wf2 = sb("wf2", [128, 4, DIM])
        w1 = sb("w1", [DIM, FF_HIDDEN])
        w2 = sb("w2", [128, 4, DIM])
        bp = sb("bp", [128, 8])
        b1 = sb("b1", [128, 4])
        norm = {n: (sb(f"{n}_g", [DIM, 1]), sb(f"{n}_b", [DIM, 1])) for n in ("ln1", "ln2", "ln3", "L1_ln", "L2_ln")}
        bias = {n: sb(f"bias_{n}", [128, DIM]) for n in ("L0a", "L0b", "L0ff", "L1", "L1ff", "L2", "L3")}
        minus_half = sb("minus_half", [128, 1])
        eps = sb("eps", [128, 1])

        loaded = {g: sem(f"loaded_{g}") for g in ("x", "ctx", "L0a", "L0b", "L0ff", "L1", "L2", "L3")}
        stored = sem("stored")
        loads = dict.fromkeys(loaded, 0)

        def load(queue, group, dst, src):
            loads[group] += 16
            queue.dma_start(dst, src).then_inc(loaded[group], 16)

        def column(v):
            return v.rearrange("(p a) -> p a", a=1)

        x_dram = a["x"].rearrange("b p d -> p b d")
        out_dram = out.rearrange("b p d -> p b d")

        def load_wide(queue, layer, q, k, v, o, bo, g, b, dkv):
            load(queue, layer, W[layer, "q"][:, :], q)
            load(queue, layer, W[layer, "k"][0:dkv, :], k)
            load(queue, layer, norm[g][0][:, :], column(a[b[0]]))
            load(queue, layer, norm[g][1][:, :], column(a[b[1]]))
            load(queue, layer, W[layer, "v"][0:dkv, :], v)
            load(queue, layer, W[layer, "o"][:, :, :], o.rearrange("(c p) n -> p c n", p=128))
            load(queue, layer, bias[layer][:, :], bo.partition_broadcast(128))

        with ExitStack() as work, nc.allow_non_contiguous_dma(reason="a few hundred bias elements, once"):
            ctx_rows = work.enter_context(nc.sbuf_tensor("ctx_rows", [TOKENS, BATCHES, CTX], FP32))
            banks = work.enter_context(nc.psum_tensor("setup_banks", [128, 8, BANK], FP32))
            ident_zero = sem("ident_zero")
            ident_ready = sem("ident_ready")
            mask_ready = sem("mask_ready")
            consts_ready = sem("consts_ready")
            ctx_bank_full = sem("ctx_bank_full")
            ctx_bank_copied = sem("ctx_bank_copied")
            w3_bank_full = sem("w3_bank_full")
            w3_copied = sem("w3_copied")
            block = work.enter_context(nc.Block())

            @block.sync
            def _(sp):
                load(sp, "x", x[:, :, :], x_dram)
                load(sp, "ctx", ctx_rows[:, :, :], a["ctx_768"].rearrange("b p d -> p b d"))
                load_wide(sp, "L0b", a["L0_xattn_Wq2"], a["L0_xattn_Wk2"], a["L0_xattn_Wv2"], a["L0_xattn_Wo2"],
                          a["L0_xattn_bo2"], "ln2", ("L0_xattn_ln2_g", "L0_xattn_ln2_b"), CTX)
                load(sp, "L0ff", wp[:, :], a["L0_xattn_Wp"])
                load(sp, "L0ff", wf2[:, :, :], a["L0_xattn_Wf2"].rearrange("(c p) n -> p c n", p=128))
                load(sp, "L0ff", bp[:, :], a["L0_xattn_bp"].rearrange("(c p) -> p c", p=128))
                load(sp, "L0ff", bias["L0ff"][:, :], a["L0_xattn_bf2"].partition_broadcast(128))
                load(sp, "L0ff", norm["ln3"][0][:, :], column(a["L0_xattn_ln3_g"]))
                load(sp, "L0ff", norm["ln3"][1][:, :], column(a["L0_xattn_ln3_b"]))
                load_wide(sp, "L2", a["L2_xattn_Wq"], a["L2_xattn_Wk"], a["L2_xattn_Wv"], a["L2_xattn_Wo"],
                          a["L2_xattn_bo"], "L2_ln", ("L2_xattn_gamma", "L2_xattn_beta"), CTX)

            @block.scalar
            def _(act):
                for w in ("q", "k", "v", "o"):
                    src = a[f"L3_xattn_W{w}"]
                    load(act, "L3", W["L3", w][:, 0:src.shape[1]], src)
                load(act, "L3", bias["L3"][:, :], a["L3_xattn_bo"].partition_broadcast(128))
                load(act, "L1", W["L1", "q"][:, :], a["L1_xattn_Wq"])
                for w in ("k", "v"):
                    load(act, "L1", W["L1", w][0:CTX, :], a[f"L1_xattn_W{w}"])
                    load(act, "L1", W["L1", w][ones_row:ones_row + 1, :],
                         a[f"L1_xattn_b{w}"].rearrange("(a n) -> a n", a=1))
                load(act, "L1", W["L1", "o"][:, :], a["L1_xattn_Wo"])
                load(act, "L1", bias["L1"][:, :], a["L1_xattn_bo"].partition_broadcast(128))
                load(act, "L1", bq[:, :], column(a["L1_xattn_bq"]))
                load_wide(act, "L0a", a["L0_xattn_Wq1"], a["L0_xattn_Wk1"], a["L0_xattn_Wv1"], a["L0_xattn_Wo1"],
                          a["L0_xattn_bo1"], "ln1", ("L0_xattn_ln1_g", "L0_xattn_ln1_b"), DIM)
                load(act, "L1", w1[:, :], a["L1_xattn_W1"])
                load(act, "L1", w2[:, :, :], a["L1_xattn_W2"].rearrange("(c p) n -> p c n", p=128))
                load(act, "L1", b1[:, :], a["L1_xattn_b1"].rearrange("(c p) -> p c", p=128))
                load(act, "L1", bias["L1ff"][:, :], a["L1_xattn_b2"].partition_broadcast(128))
                load(act, "L1", norm["L1_ln"][0][:, :], column(a["L1_xattn_ln_g"]))
                load(act, "L1", norm["L1_ln"][1][:, :], column(a["L1_xattn_ln_b"]))

            @block.gpsimd
            def _(pool):
                nc.gpsimd.memset(ident[:, :], 0.0).then_inc(ident_zero, 1)
                pool.wait_ge(ident_zero, 1)
                nc.gpsimd.affine_select(out=ident[:, :], in_=ident[:, :], compare_op=ALU.not_equal, fill=1.0,
                                        base=0, pattern=[[-1, 128]], channel_multiplier=1).then_inc(ident_ready, 1)
                pool.wait_ge(ident_ready, 1)
                nc.gpsimd.memset(ctxT[ones_row:ones_row + 1, :, :], 1.0).then_inc(consts_ready, 1)
                pool.wait_ge(consts_ready, 1)
                nc.gpsimd.memset(minus_half[:, :], -0.5).then_inc(consts_ready, 1)
                nc.gpsimd.memset(eps[:, :], EPS).then_inc(consts_ready, 1)
                pool.wait_ge(consts_ready, 3)
                nc.gpsimd.memset(head_mask[:, :], 1.0).then_inc(mask_ready, 1)
                steps = 1
                for lo in (0, 64):
                    for base, sign in ((0, 1), (NARROW - 1, -1)):
                        pool.wait_ge(mask_ready, steps)
                        part = head_mask[lo:lo + 64, :]
                        nc.gpsimd.affine_select(out=part, in_=part, compare_op=ALU.is_ge, fill=0.0, base=base,
                                                pattern=[[-NARROW * sign, SLOT_HEADS]],
                                                channel_multiplier=sign).then_inc(mask_ready, 1)
                        steps += 1
                pool.wait_ge(mask_ready, steps)

            @block.vector
            def _(dve):
                for n, (w, rows) in enumerate((("q", DIM), ("k", CTX), ("v", CTX), ("o", DIM))):
                    dve.wait_ge(w3_bank_full, n + 1)
                    src = banks[0:rows, n, 0:DIM]
                    nc.vector.tensor_copy(W["L3", w + "T"][0:rows, :], src).then_inc(w3_copied, 1)
                for n in range(BATCHES // 4):
                    dve.wait_ge(ctx_bank_full, n + 1)
                    nc.vector.tensor_copy(ctxT[0:CTX, 4 * n:4 * n + 4, :],
                                          banks[0:CTX, 4 + n % 4, :].rearrange("p (b t) -> p b t", b=4)
                                          ).then_inc(ctx_bank_copied, 1)
                dve.wait_ge(ctx_bank_copied, BATCHES // 4)

            @block.tensor
            def _(pe):
                pe.wait_ge(ident_ready, 1)
                pe.wait_ge(loaded["L3"], 16 * 5)
                for n, (w, cols) in enumerate((("q", DIM), ("k", CTX), ("v", CTX), ("o", DIM))):
                    nc.tensor.transpose(banks[0:cols, n, 0:DIM], W["L3", w][:, 0:cols],
                                        ident[:, :]).then_inc(w3_bank_full, 1)
                pe.wait_ge(loaded["ctx"], 16)
                for n in range(BATCHES // 4):
                    if n >= 4:
                        pe.wait_ge(ctx_bank_copied, n - 3)
                    for k in range(4):
                        last = nc.tensor.transpose(banks[0:CTX, 4 + n % 4, 128 * k:128 * k + 128],
                                                   ctx_rows[:, 4 * n + k, :], ident[:, :])
                    last.then_inc(ctx_bank_full, 1)

        attention(nc, "L0a", x, x, None, W["L0a", "q"], W["L0a", "k"], W["L0a", "v"], W["L0a", "o"],
                  ident, minus_half, eps, bias["L0a"], norm["ln1"], head=WIDE, kv_rows=DIM, scale=WIDE ** -0.5,
                  waits=[(loaded["x"], 16), (loaded["L0a"], loads["L0a"])])
        attention(nc, "L0b", x, x, ctxT, W["L0b", "q"], W["L0b", "k"], W["L0b", "v"], W["L0b", "o"],
                  ident, minus_half, eps, bias["L0b"], norm["ln2"], head=WIDE, kv_rows=CTX, scale=WIDE ** -0.5,
                  waits=[(loaded["L0b"], loads["L0b"])])
        feed_forward(nc, "L0ff", x, x, wp, wf2, bp, bias["L0ff"], norm["ln3"], ident, minus_half, eps, gated=True,
                     waits=[(loaded["L0ff"], loads["L0ff"])])
        with nc.sbuf_tensor("y", [TOKENS, BATCHES, DIM], FP32) as y:
            attention(nc, "L1", x, y, ctxT, W["L1", "q"], W["L1", "k"], W["L1", "v"], W["L1", "o"],
                      ident, minus_half, eps, bias["L1"], None, head=NARROW, kv_rows=CTX + 1, scale=NARROW ** -0.5,
                      waits=[(loaded["L1"], loads["L1"])], q_bias=bq, head_mask=head_mask)
            feed_forward(nc, "L1ff", x, y, w1, w2, b1, bias["L1ff"], norm["L1_ln"], ident, minus_half, eps, gated=False,
                         waits=[(loaded["L1"], loads["L1"])])
        attention(nc, "L2", x, x, ctxT, W["L2", "q"], W["L2", "k"], W["L2", "v"], W["L2", "o"],
                  ident, minus_half, eps, bias["L2"], norm["L2_ln"], head=WIDE, kv_rows=CTX, scale=1.0,
                  out_scale=WIDE ** -0.5, waits=[(loaded["L2"], loads["L2"])])
        attention(nc, "L3", x, x, ctxT, W["L3", "qT"], W["L3", "kT"], W["L3", "vT"], W["L3", "oT"],
                  ident, minus_half, eps, bias["L3"], None, head=NARROW, kv_rows=CTX, scale=NARROW ** -0.5,
                  waits=[(loaded["L3"], loads["L3"])], head_mask=head_mask, store=(out_dram, stored))


def attention(nc, layer, x, dst, ctxT, wq, wk, wv, wo, ident, minus_half, eps, bias_o, norm, *, head, kv_rows,
              scale, waits, q_bias=None, head_mask=None, out_scale=1.0, store=None):
    wide = head == WIDE
    residual = dst is x
    self_attention = ctxT is None
    if wide:
        order = [("Wo", -1, "dve"), ("T0", 0, "act"), ("T1", 0, "act"), ("q0", 2, "act"), ("k0", 2, "act"),
                 ("PV0", 0, "dve"), ("T2", 0, "act"), ("T3", 0, "act"), ("q1", 2, "act"), ("k1", 2, "act"),
                 ("v0", 1, "act"), ("v1", 1, "act"), ("hT", 3, "dve"), ("PV1", 0, "dve")]
    else:
        order = [("Wo", -1, "dve"), ("T0", 0, "act"), ("T1", 0, "act"), ("qk", 2, "act"), ("T2", 0, "act"),
                 ("T3", 0, "act"), ("v0", 1, "act"), ("iT", 0, "act"), ("hT", 3, "dve"), ("PV0", 0, "dve")]
    first, last = -4, BATCHES
    steady_first, steady_last = 3, BATCHES - 5
    ring = Ring(order, range(first, last + 1), BATCHES)
    chunks = INNER // 128
    half_rows = 64
    last_v, last_pv = ("v1", "PV1") if wide else ("v0", "PV0")
    GROUP = 4
    QUAD = DIM // 4
    SKEW = QUAD + NARROW

    def here(at, lag):
        return 0 <= at.n + lag < BATCHES

    with ExitStack() as ctx:
        def sb(name, shape):
            return ctx.enter_context(nc.sbuf_tensor(f"{layer}_{name}", shape, FP32))

        def sem(name):
            return ctx.enter_context(nc.semaphore(f"{layer}_{name}"))

        rows_h = sb("rows_h", [TOKENS, DIM])
        hT = sb("hT", [DIM, 2, TOKENS])
        cT = None if self_attention else sb("cT", [kv_rows, 2, TOKENS])
        if wide:
            qT = sb("qT", [128, 2, chunks, TOKENS])
            kT = sb("kT", [128, 2, chunks, TOKENS])
            v = sb("v", [TOKENS, 2, INNER])
            oT = sb("oT", [128, chunks, TOKENS])
        else:
            qT = sb("qT", [128, 2, TOKENS])
            kT = sb("kT", [128, 2, TOKENS])
            k_apart = sb("k_apart", [128, 2, SLOT_HEADS, TOKENS])
            v = sb("v", [TOKENS, 2, 4, 4 * SKEW])
            oT = sb("oT", [128, 1, TOKENS])
            inv_wide = sb("inv_wide", [TOKENS, 2, HEADS, NARROW])
            invT = sb("invT", [128, TOKENS])
        probs = sb("probs", [TOKENS, 2, SLOT_HEADS, TOKENS])
        probsT = sb("probsT", [TOKENS, HEADS, TOKENS])
        x_bias = sb("x_bias", [TOKENS, 2, DIM]) if residual else None
        stats = sb("stats", [TOKENS, 2, 6])
        wait_carrier = sb("wait_carrier", [TOKENS, 1])
        moments = sb("moments", [TOKENS, 2, 2])
        var_eps = sb("var_eps", [TOKENS, 2, 1])
        rstd = sb("rstd", [TOKENS, 2, 1])
        row_max = sb("row_max", [TOKENS, 2, SLOT_HEADS])
        neg_max = sb("neg_max", [TOKENS, SLOT_HEADS])
        sums = sb("sums", [TOKENS, 2, 2, GROUP])
        inv_sum = sb("inv_sum", [TOKENS, 2, 2, GROUP])
        scores = ctx.enter_context(nc.psum_tensor(f"{layer}_scores", [TOKENS, 2, 2, GROUP, TOKENS], FP32))
        ring_banks = ctx.enter_context(nc.psum_tensor(f"{layer}_ring", [128, Ring.BANKS, BANK], FP32))

        filled = {"act": sem("ring_filled_act"), "dve": sem("ring_filled_dve")}
        emptied = {"act": sem("ring_emptied_act"), "dve": sem("ring_emptied_dve")}
        if norm is not None:
            stats_ready, moments_ready = sem("stats_ready"), sem("moments_ready")
            var_ready, rstd_ready = sem("var_ready"), sem("rstd_ready")
        rows_h_ready = sem("rows_h_ready")
        if not self_attention:
            cT_ready = sem("cT_ready")
        if residual:
            x_bias_ready = sem("x_bias_ready")
        scores_full = [sem("scores_full_0"), sem("scores_full_1")]
        max_ready = [sem("max_ready_0"), sem("max_ready_1")]
        neg_max_ready = sem("neg_max_ready")
        shifted = sem("shifted")
        exp_ready = [sem("exp_ready_0"), sem("exp_ready_1")]
        sum_ready = sem("sum_ready")
        inverted = [sem("inverted_0"), sem("inverted_1")]
        if wide:
            divided = sem("divided")
        else:
            v_cleared = sem("v_cleared")
            keys_apart = sem("keys_apart")
            inv_wide_ready = sem("inv_wide_ready")
        block = ctx.enter_context(nc.Block())

        def bank(name, at):
            return ring_banks[:, ring.bank(name, at), :]

        def await_filled(engine, name, at):
            engine.wait_ge(filled[ring.engine[name]], ring.count(name, at))

        def await_emptied(engine, name, at):
            engine.wait_ge(emptied[ring.engine[name]], ring.count(name, at))

        def steps(engine, step):
            pipeline(engine, step, first, last, steady_first, steady_last)

        @block.tensor
        def _(pe):
            for semaphore, value in waits:
                pe.wait_ge(semaphore, value)

            def start_fill(name, at):
                before = ring.before(name, at)
                if before:
                    pe.wait_ge(emptied[before[0]], before[1])
                return bank(name, at)

            def filled_by(instruction, name):
                instruction.then_inc(filled[ring.engine[name]], 1)

            def score(at, s):
                p = at.n % 2
                if wide:
                    await_emptied(pe, f"q{s}", at)
                    await_emptied(pe, f"k{s}", at)
                else:
                    pe.wait_ge(keys_apart, at.times(1, 1))
                if at.n >= 1:
                    if s == 0:
                        pe.wait_ge(exp_ready[0], at.times(1, 0))
                    else:
                        pe.wait_ge(shifted, at.times(1, 0))
                for i in range(GROUP if wide else 1):
                    for r in range(2):
                        part = slice(half_rows * r, half_rows * (r + 1))
                        if wide:
                            c = GROUP * s + i
                            to, q, k = scores[:, s, r, i, :], qT[part, p, c, :], kT[part, p, c, :]
                        else:
                            to, q = scores[:, s, r, :, :], qT[part, p, :]
                            k = k_apart[part, p, GROUP * s:GROUP * (s + 1), :]
                        last = nc.tensor.matmul(to, q, k, start=True, stop=True, tile_position=(half_rows * r, 0))
                last.then_inc(scores_full[s], 1)

            def transpose_probs(at, n):
                s, r = divmod(n, 2)
                if r == 0:
                    if wide:
                        pe.wait_ge(divided, at.times(2, s + 1))
                    else:
                        pe.wait_ge(exp_ready[s], at.times(1, 1))
                to = start_fill(f"T{n}", at)
                for i in range(GROUP):
                    last = nc.tensor.transpose(to[:, TOKENS * i:TOKENS * (i + 1)], probs[:, s, GROUP * r + i, :],
                                               ident[:, :])
                filled_by(last, f"T{n}")

            def project_T(name, at, w, src, src_rows, n):
                to = start_fill(name, at)
                for c in range(4):
                    last = nc.tensor.matmul(to[:, TOKENS * c:TOKENS * (c + 1)],
                                            w[0:src_rows, BANK * n + 128 * c:BANK * n + 128 * (c + 1)],
                                            src, start=True, stop=True)
                filled_by(last, name)

            def await_kv_source(at):
                if not self_attention:
                    pe.wait_ge(cT_ready, at.times(1, 1))

            def kv_source(at):
                return (hT if self_attention else cT)[0:kv_rows, at.n % 2, :]

            def queries_keys(at, n):
                if n == 0:
                    await_emptied(pe, "hT", at)
                    await_kv_source(at)
                if wide:
                    project_T(f"q{n}", at, wq, hT[:, at.n % 2, :], DIM, n)
                    project_T(f"k{n}", at, wk, kv_source(at), kv_rows, n)
                else:
                    to = start_fill("qk", at)
                    nc.tensor.matmul(to[:, 0:TOKENS], wq[:, :], hT[:, at.n % 2, :], start=True, stop=True)
                    filled_by(nc.tensor.matmul(to[:, TOKENS:2 * TOKENS], wk[0:kv_rows, :], kv_source(at),
                                               start=True, stop=True), "qk")

            def values(at, n):
                to = start_fill(f"v{n}", at)
                cols = BANK if wide else DIM
                filled_by(nc.tensor.matmul(to[:, 0:cols], kv_source(at), wv[0:kv_rows, cols * n:cols * (n + 1)],
                                           start=True, stop=True), f"v{n}")

            def weigh_wide(at, s):
                if s == 0:
                    await_emptied(pe, last_v, at)
                await_emptied(pe, f"T{2 * s + 1}", at)
                to = start_fill(f"PV{s}", at)
                for i in range(GROUP):
                    for r in range(2):
                        h = 2 * (GROUP * s + i) + r
                        last = nc.tensor.matmul(to[WIDE * r:WIDE * (r + 1), TOKENS * i:TOKENS * (i + 1)],
                                                v[:, at.n % 2, WIDE * h:WIDE * (h + 1)],
                                                probsT[:, SLOT_HEADS * s + GROUP * r + i, :],
                                                start=True, stop=True, tile_position=(0, WIDE * r))
                filled_by(last, f"PV{s}")

            def weigh_narrow(at):
                await_emptied(pe, last_v, at)
                await_emptied(pe, "T3", at)
                to = start_fill("PV0", at)
                for j in range(4):
                    for g in range(4):
                        r, s = divmod(g, 2)
                        last = nc.tensor.matmul(to[QUAD * g:QUAD * (g + 1), 0:TOKENS],
                                                v[:, at.n % 2, g, QUAD * j:QUAD * (j + 1)],
                                                probsT[:, SLOT_HEADS * s + GROUP * r + j, :],
                                                start=j == 0, stop=j == 3, tile_position=(0, QUAD * g))
                filled_by(last, "PV0")

            def transpose_inverses(at):
                pe.wait_ge(inv_wide_ready, at.times(1, 1))
                filled_by(nc.tensor.transpose(start_fill("iT", at)[:, 0:TOKENS],
                                              inv_wide[:, at.n % 2, :, :].rearrange("p h d -> p (h d)"),
                                              ident[:, :]), "iT")

            def transpose_h(at):
                pe.wait_ge(rows_h_ready, at.times(1, 1))
                filled_by(nc.tensor.transpose(start_fill("hT", at)[:, 0:TOKENS], rows_h[:, :], ident[:, :]), "hT")

            def project_out(at):
                await_emptied(pe, last_pv, at)
                to = start_fill("Wo", at)
                pieces = chunks if wide else 1
                for c in range(pieces):
                    w = wo[:, c, :] if wide else wo[:, :]
                    last = nc.tensor.matmul(to[:, 0:DIM], oT[:, c, :], w, start=c == 0, stop=c == pieces - 1)
                filled_by(last, "Wo")

            def step(t):
                if here(t, 1):
                    score(t.plus(1), 0)
                if here(t, -1):
                    project_out(t.plus(-1))
                if here(t, 0):
                    transpose_probs(t, 0)
                    transpose_probs(t, 1)
                if here(t, 2):
                    queries_keys(t.plus(2), 0)
                if wide and here(t, 0):
                    weigh_wide(t, 0)
                if here(t, 1):
                    score(t.plus(1), 1)
                if here(t, 0):
                    transpose_probs(t, 2)
                    transpose_probs(t, 3)
                if wide and here(t, 2):
                    queries_keys(t.plus(2), 1)
                if here(t, 1):
                    values(t.plus(1), 0)
                    if wide:
                        values(t.plus(1), 1)
                if not wide and here(t, 0):
                    transpose_inverses(t)
                if here(t, 3):
                    transpose_h(t.plus(3))
                if here(t, 0):
                    if wide:
                        weigh_wide(t, 1)
                    else:
                        weigh_narrow(t)

            steps(pe, step)

        @block.scalar
        def _(act):
            if not wide:
                act.wait_ge(v_cleared, 1)

            def copied(to, src):
                nc.scalar.activation(to, src, ACT.Copy).then_inc(emptied["act"], 1)

            def exponentiate(at, s):
                if s == 0:
                    act.wait_ge(neg_max_ready, at.times(1, 1))
                    if at.n >= 1:
                        act.wait_ge(inverted[0], at.times(1, 0))
                    for n in range(SLOT_HEADS):
                        r, i = divmod(n, GROUP)
                        done = nc.scalar.activation(probs[:, 0, n, :], scores[:, 0, r, i, :], ACT.Exp, scale=scale,
                                                    bias=neg_max[:, n:n + 1], accum_out=sums[:, r, 0, i:i + 1])
                    done.then_inc(exp_ready[0], 1)
                else:
                    act.wait_ge(shifted, at.times(1, 1))
                    nc.scalar.activation(probs[:, 1, :, :], probs[:, 1, :, :], ACT.Exp,
                                         scale=scale).then_inc(exp_ready[1], 1)

            def projections(at, n):
                p = at.n % 2
                if wide:
                    for name, to in ((f"q{n}", qT), (f"k{n}", kT)):
                        await_filled(act, name, at)
                        copied(to[:, p, 4 * n:4 * n + 4, :].rearrange("p c t -> p (c t)"), bank(name, at))
                else:
                    await_filled(act, "qk", at)
                    if at.n >= 2:
                        act.wait_ge(keys_apart, at.times(1, -1))
                    src = bank("qk", at)
                    if q_bias is None:
                        nc.scalar.activation(qT[:, p, :], src[:, 0:TOKENS], ACT.Copy)
                    else:
                        nc.scalar.activation(qT[:, p, :], src[:, 0:TOKENS], ACT.Identity, bias=q_bias[:, :])
                    copied(kT[:, p, :], src[:, TOKENS:2 * TOKENS])

            def values(at):
                if wide:
                    for n in range(2):
                        await_filled(act, f"v{n}", at)
                        copied(v[:, at.n % 2, BANK * n:BANK * (n + 1)], bank(f"v{n}", at))
                else:
                    await_filled(act, "v0", at)
                    copied(v[:, at.n % 2, :, :].rearrange("p g (j k) -> p g j k", k=SKEW)[:, :, :, 0:NARROW],
                           bank("v0", at)[:, 0:DIM].rearrange("p (g j d) -> p g j d", j=4, d=NARROW))

            def turned_probs(at, n):
                await_filled(act, f"T{n}", at)
                copied(probsT[:, GROUP * n:GROUP * (n + 1), :].rearrange("p h t -> p (h t)"), bank(f"T{n}", at))

            def step(t):
                if here(t, 0):
                    turned_probs(t, 0)
                    turned_probs(t, 1)
                if here(t, 2):
                    projections(t.plus(2), 0)
                if here(t, 1):
                    exponentiate(t.plus(1), 0)
                if here(t, 0):
                    turned_probs(t, 2)
                    turned_probs(t, 3)
                if wide and here(t, 2):
                    projections(t.plus(2), 1)
                if here(t, 1):
                    exponentiate(t.plus(1), 1)
                    values(t.plus(1))
                if not wide and here(t, 0):
                    await_filled(act, "iT", t)
                    copied(invT[:, :], bank("iT", t)[:, 0:TOKENS])

            steps(act, step)

        @block.vector
        def _(dve):
            if not wide:
                nc.vector.memset(v[:, :, :, :], 0.0).then_inc(v_cleared, 1)
            for semaphore, value in waits:
                dve.wait_ge(semaphore, value)

            def statistics(at):
                p = at.n % 2
                nc.vector.bn_stats(stats[:, p, :], x[:, at.index, :]).then_inc(stats_ready, 1)
                dve.wait_ge(stats_ready, at.times(1, 1))
                nc.vector.memset(wait_carrier[:, :], 0.0)
                nc.vector.bn_aggr(moments[:, p, :], stats[:, p, :]).then_inc(moments_ready, 1)

            def normalise(at):
                p = at.n % 2
                dve.wait_ge(moments_ready, at.times(1, 1))
                dve.wait_ge(rstd_ready, at.times(1, 1))
                if at.n >= 1:
                    await_filled(dve, "hT", at.plus(-1))
                nc.vector.tensor_scalar(rows_h[:, :], x[:, at.index, :], moments[:, p, 0:1], rstd[:, p, :],
                                        ALU.subtract, ALU.mult).then_inc(rows_h_ready, 1)

            def slot(s):
                return scores[:, s, :, :, :].rearrange("p r i k -> p (r i) k")

            def row_maxima(at, s):
                dve.wait_ge(scores_full[s], at.times(1, 1))
                nc.vector.tensor_reduce(row_max[:, s, :], slot(s), AX.X, ALU.max).then_inc(max_ready[s], 1)
                dve.wait_ge(max_ready[s], at.times(1, 1))

            def negate_maxima(at):
                if at.n >= 1:
                    dve.wait_ge(exp_ready[0], at.times(1, 0))
                nc.vector.tensor_scalar(neg_max[:, :], row_max[:, 0, :], -scale, None,
                                        ALU.mult).then_inc(neg_max_ready, 1)

            def subtract_maxima(at):
                if at.n >= 1:
                    await_filled(dve, "T3", at.plus(-1))
                nc.vector.tensor_tensor(probs[:, 1, :, :], slot(1),
                                        row_max[:, 1, :].unsqueeze(2).to_broadcast([TOKENS, SLOT_HEADS, TOKENS]),
                                        ALU.subtract).then_inc(shifted, 1)

            def add_up(at):
                dve.wait_ge(exp_ready[1], at.times(1, 1))
                nc.vector.tensor_reduce(sums[:, :, 1, :], probs[:, 1, :, :].rearrange("p (r i) k -> p r i k", r=2),
                                        AX.X, ALU.add).then_inc(sum_ready, 1)

            def invert(at, s):
                if s == 0:
                    dve.wait_ge(exp_ready[0], at.times(1, 1))
                else:
                    dve.wait_ge(sum_ready, at.times(1, 1))
                if wide and at.n >= 1:
                    dve.wait_ge(divided, at.times(2, s - 1))
                nc.vector.reciprocal(inv_sum[:, :, s, :], sums[:, :, s, :]).then_inc(inverted[s], 1)

            def repeat_inverses(at):
                dve.wait_ge(inverted[1], at.times(1, 1))
                nc.vector.tensor_copy(inv_wide[:, at.n % 2, :, :],
                                      inv_sum[:, :, :, :].rearrange("p r s i -> p (r s i)").unsqueeze(2)
                                      .to_broadcast([TOKENS, HEADS, NARROW])).then_inc(inv_wide_ready, 1)

            def weighted_wide(at, s):
                await_filled(dve, f"PV{s}", at)
                nc.vector.tensor_copy(oT[:, GROUP * s:GROUP * (s + 1), :].rearrange("p c t -> p (c t)"),
                                      bank(f"PV{s}", at)).then_inc(emptied["dve"], 1)

            def weighted_narrow(at):
                await_emptied(dve, "iT", at)
                await_filled(dve, "PV0", at)
                nc.vector.tensor_tensor(oT[:, 0, :], bank("PV0", at)[:, 0:TOKENS], invT[:, :],
                                        ALU.mult).then_inc(emptied["dve"], 1)

            def turned_h(at):
                await_filled(dve, "hT", at)
                src = bank("hT", at)[:, 0:TOKENS]
                if norm is None:
                    nc.vector.tensor_copy(hT[:, at.n % 2, :], src).then_inc(emptied["dve"], 1)
                else:
                    nc.vector.tensor_scalar(hT[:, at.n % 2, :], src, norm[0][:, :], norm[1][:, :],
                                            ALU.mult, ALU.add).then_inc(emptied["dve"], 1)

            def finish(at):
                await_filled(dve, "Wo", at)
                if residual:
                    dve.wait_ge(x_bias_ready, at.times(1, 1))
                    plus = x_bias[:, at.n % 2, :]
                else:
                    plus = bias_o[:, :]
                src = bank("Wo", at)[:, 0:DIM]
                if out_scale == 1.0:
                    done = nc.vector.tensor_tensor(dst[:, at.index, :], src, plus, ALU.add)
                else:
                    done = nc.vector.scalar_tensor_tensor(dst[:, at.index, :], src, out_scale, plus,
                                                          ALU.mult, ALU.add)
                done.then_inc(emptied["dve"], 1)

            def step(t):
                if here(t, 1):
                    row_maxima(t.plus(1), 0)
                    negate_maxima(t.plus(1))
                if here(t, -1):
                    finish(t.plus(-1))
                if norm is not None and here(t, 4):
                    statistics(t.plus(4))
                if wide and here(t, 0):
                    weighted_wide(t, 0)
                if norm is not None and here(t, 3):
                    normalise(t.plus(3))
                if here(t, 1):
                    row_maxima(t.plus(1), 1)
                    subtract_maxima(t.plus(1))
                    invert(t.plus(1), 0)
                if here(t, 3):
                    turned_h(t.plus(3))
                if here(t, 0):
                    if wide:
                        weighted_wide(t, 1)
                    else:
                        weighted_narrow(t)
                if here(t, 1):
                    add_up(t.plus(1))
                    invert(t.plus(1), 1)
                    if not wide:
                        repeat_inverses(t.plus(1))

            steps(dve, step)

        @block.gpsimd
        def _(pool):
            for semaphore, value in waits:
                pool.wait_ge(semaphore, value)

            def inverse_deviation(at):
                p = at.n % 2
                pool.wait_ge(moments_ready, at.times(1, 1))
                if at.n >= 2:
                    pool.wait_ge(rows_h_ready, at.times(1, -1))
                nc.gpsimd.tensor_tensor(var_eps[:, p, :], moments[:, p, 1:2], eps[:, :], ALU.add).then_inc(var_ready, 1)
                pool.wait_ge(var_ready, at.times(1, 1))
                nc.gpsimd.tensor_tensor(rstd[:, p, :], var_eps[:, p, :], minus_half[:, :],
                                        ALU.pow).then_inc(rstd_ready, 1)

            def copy_rows(at):
                if at.n >= 1:
                    await_filled(pool, "hT", at.plus(-1))
                nc.gpsimd.tensor_copy(rows_h[:, :], x[:, at.index, :]).then_inc(rows_h_ready, 1)

            def add_bias(at):
                if at.n >= 2:
                    await_emptied(pool, "Wo", at.plus(-2))
                nc.gpsimd.tensor_tensor(x_bias[:, at.n % 2, :], x[:, at.index, :], bias_o[:, :],
                                        ALU.add).then_inc(x_bias_ready, 1)

            def stage_context(at):
                if at.n >= 2:
                    await_filled(pool, last_v, at.plus(-2))
                nc.gpsimd.tensor_copy(cT[0:kv_rows, at.n % 2, :],
                                      ctxT[0:kv_rows, at.index, :]).then_inc(cT_ready, 1)

            def set_keys_apart(at):
                p = at.n % 2
                await_emptied(pool, "qk", at)
                nc.gpsimd.tensor_tensor(k_apart[:, p, :, :],
                                        kT[:, p, :].unsqueeze(1).to_broadcast([128, SLOT_HEADS, TOKENS]),
                                        head_mask[:, :].unsqueeze(2).to_broadcast([128, SLOT_HEADS, TOKENS]),
                                        ALU.mult).then_inc(keys_apart, 1)

            def divide(at, s):
                pool.wait_ge(inverted[s], at.times(1, 1))
                to = probs[:, s, :, :].rearrange("p (r i) k -> p r i k", r=2)
                nc.gpsimd.tensor_tensor(to, to, inv_sum[:, :, s, :].unsqueeze(3)
                                        .to_broadcast([TOKENS, 2, GROUP, TOKENS]), ALU.mult).then_inc(divided, 1)

            def step(t):
                if norm is not None and here(t, 4):
                    inverse_deviation(t.plus(4))
                if norm is None and here(t, 3):
                    copy_rows(t.plus(3))
                if residual and here(t, 1):
                    add_bias(t.plus(1))
                if not wide and here(t, 2):
                    set_keys_apart(t.plus(2))
                if wide and here(t, 1):
                    divide(t.plus(1), 0)
                if not self_attention and here(t, 3):
                    stage_context(t.plus(3))
                if wide and here(t, 1):
                    divide(t.plus(1), 1)

            steps(pool, step)

        if store is not None:
            @block.sync
            def _(sp):
                out_dram, stored = store
                for b in range(BATCHES):
                    await_emptied(sp, "Wo", At(b))
                    sp.dma_start(out_dram[:, b, :], dst[:, b, :]).then_inc(stored, 16)
                sp.wait_ge(stored, 16 * BATCHES)


def feed_forward(nc, layer, x, src, w_in, w_out, b_in, bias_out, norm, ident, minus_half, eps, *, gated, waits):
    SIZE = 4
    GROUPS = BATCHES // SIZE
    CHUNKS = FF_HIDDEN // 128
    add_src = src is not x

    def here(at, lag):
        return 0 <= at.n + lag < GROUPS

    with ExitStack() as ctx:
        def sb(name, shape):
            return ctx.enter_context(nc.sbuf_tensor(f"{layer}_{name}", shape, FP32))

        def sem(name):
            return ctx.enter_context(nc.semaphore(f"{layer}_{name}"))

        stats = sb("stats", [TOKENS, SIZE, 6])
        wait_carrier = sb("wait_carrier", [TOKENS, 1])
        moments = sb("moments", [TOKENS, SIZE, 2])
        var_eps = sb("var_eps", [TOKENS, SIZE])
        rstd = sb("rstd", [TOKENS, SIZE])
        rows_h = sb("rows_h", [TOKENS, SIZE, DIM])
        hT = sb("hT", [DIM, 2, SIZE * TOKENS])
        gelu = sb("gelu", [128, 2, SIZE * TOKENS]) if gated else None
        hidden = sb("hidden", [128, 2, CHUNKS, SIZE * TOKENS])
        base = sb("base", [TOKENS, 2, SIZE, DIM])
        in_banks = ctx.enter_context(nc.psum_tensor(f"{layer}_in", [128, 4, BANK], FP32))
        out_banks = ctx.enter_context(nc.psum_tensor(f"{layer}_out", [128, 2, BANK], FP32))
        turn_banks = ctx.enter_context(nc.psum_tensor(f"{layer}_turn", [128, 2, BANK], FP32))

        stats_ready = sem("stats_ready")
        moments_ready = sem("moments_ready")
        var_ready = sem("var_ready")
        rstd_ready = sem("rstd_ready")
        rows_ready = sem("rows_ready")
        turned = sem("turned")
        hT_ready = sem("hT_ready")
        gate_full = sem("gate_full")
        if gated:
            value_full, gelu_ready = sem("value_full"), sem("gelu_ready")
        hidden_ready = sem("hidden_ready")
        out_full = sem("out_full")
        out_added = sem("out_added")
        if add_src:
            base_sum = sem("base_sum")
        base_ready = sem("base_ready")
        block = ctx.enter_context(nc.Block())

        def steps(engine, step):
            pipeline(engine, step, -2, GROUPS - 1, 2, GROUPS - 3)

        def gate_bank(c):
            return in_banks[:, c % 2 if gated else c, :]

        @block.tensor
        def _(pe):
            for semaphore, value in waits:
                pe.wait_ge(semaphore, value)

            def transpose_rows(at):
                pe.wait_ge(rows_ready, at.times(SIZE, SIZE))
                if at.n >= 2:
                    pe.wait_ge(hT_ready, at.times(1, -1))
                for k in range(SIZE):
                    last = nc.tensor.transpose(turn_banks[:, at.n % 2, 128 * k:128 * (k + 1)], rows_h[:, k, :],
                                               ident[:, :])
                last.then_inc(turned, 1)

            def expand(at):
                pe.wait_ge(hT_ready, at.times(1, 1))
                for c in range(CHUNKS):
                    if gated:
                        before = at.times(CHUNKS, c - 1)
                        if at.n > 0 or c >= 2:
                            pe.wait_ge(gelu_ready, before)
                    elif at.n > 0:
                        pe.wait_ge(hidden_ready, at.times(CHUNKS, c - 3))
                    gate_col = FF_HIDDEN + 128 * c if gated else 128 * c
                    nc.tensor.matmul(gate_bank(c), w_in[:, gate_col:gate_col + 128], hT[:, at.n % 2, :],
                                     start=True, stop=True).then_inc(gate_full, 1)
                    if gated:
                        if at.n > 0 or c >= 2:
                            pe.wait_ge(hidden_ready, before)
                        nc.tensor.matmul(in_banks[:, 2 + c % 2, :], w_in[:, 128 * c:128 * c + 128],
                                         hT[:, at.n % 2, :], start=True, stop=True).then_inc(value_full, 1)

            def contract(at):
                pe.wait_ge(hidden_ready, at.times(CHUNKS, CHUNKS))
                if at.n >= 2:
                    pe.wait_ge(out_added, at.times(1, -1))
                for k in range(SIZE):
                    for c in range(CHUNKS):
                        last = nc.tensor.matmul(out_banks[:, at.n % 2, 128 * k:128 * (k + 1)],
                                                hidden[:, at.n % 2, c, 128 * k:128 * (k + 1)], w_out[:, c, :],
                                                start=c == 0, stop=c == CHUNKS - 1)
                last.then_inc(out_full, 1)

            def step(t):
                if here(t, 1):
                    expand(t.plus(1))
                if here(t, 2):
                    transpose_rows(t.plus(2))
                if here(t, 0):
                    contract(t)

            steps(pe, step)

        @block.scalar
        def _(act):
            for semaphore, value in waits:
                act.wait_ge(semaphore, value)

            def activate(at):
                for c in range(CHUNKS):
                    act.wait_ge(gate_full, at.times(CHUNKS, c + 1))
                    if gated:
                        if at.n > 0 or c >= 2:
                            act.wait_ge(hidden_ready, at.times(CHUNKS, c - 1))
                        nc.scalar.activation(gelu[:, c % 2, :], gate_bank(c), ACT.Gelu,
                                             bias=b_in[:, CHUNKS + c:CHUNKS + c + 1]).then_inc(gelu_ready, 1)
                    else:
                        if at.n >= 2:
                            act.wait_ge(out_full, at.times(1, -1))
                        nc.scalar.activation(hidden[:, at.n % 2, c, :], gate_bank(c), ACT.Gelu,
                                             bias=b_in[:, c:c + 1]).then_inc(hidden_ready, 1)

            def step(t):
                if here(t, 1):
                    activate(t.plus(1))

            steps(act, step)

        @block.vector
        def _(dve):
            for semaphore, value in waits:
                dve.wait_ge(semaphore, value)

            def statistics(at):
                for k in range(SIZE):
                    if k == 0 and at.n >= 1:
                        dve.wait_ge(rstd_ready, at.times(1, 0))
                    nc.vector.bn_stats(stats[:, k, :], src[:, at.times(SIZE, k), :]).then_inc(stats_ready, 1)
                for k in range(SIZE):
                    if k == 0:
                        dve.wait_ge(stats_ready, at.times(SIZE, SIZE))
                        nc.vector.memset(wait_carrier[:, :], 0.0)
                    nc.vector.bn_aggr(moments[:, k, :], stats[:, k, :]).then_inc(moments_ready, 1)

            def normalise(at):
                dve.wait_ge(moments_ready, at.times(SIZE, SIZE))
                dve.wait_ge(rstd_ready, at.times(1, 1))
                if at.n >= 1:
                    dve.wait_ge(turned, at.times(1, 0))
                for k in range(SIZE):
                    nc.vector.tensor_scalar(rows_h[:, k, :], src[:, at.times(SIZE, k), :], moments[:, k, 0:1],
                                            rstd[:, k:k + 1], ALU.subtract, ALU.mult).then_inc(rows_ready, 1)

            def scale_turned(at):
                dve.wait_ge(turned, at.times(1, 1))
                nc.vector.tensor_scalar(hT[:, at.n % 2, :], turn_banks[:, at.n % 2, :], norm[0][:, :], norm[1][:, :],
                                        ALU.mult, ALU.add).then_inc(hT_ready, 1)

            def gate(at):
                for c in range(CHUNKS):
                    dve.wait_ge(value_full, at.times(CHUNKS, c + 1))
                    dve.wait_ge(gelu_ready, at.times(CHUNKS, c + 1))
                    nc.vector.scalar_tensor_tensor(hidden[:, at.n % 2, c, :], in_banks[:, 2 + c % 2, :],
                                                   b_in[:, c:c + 1], gelu[:, c % 2, :], ALU.add,
                                                   ALU.mult).then_inc(hidden_ready, 1)

            def finish(at):
                dve.wait_ge(out_full, at.times(1, 1))
                dve.wait_ge(base_ready, at.times(SIZE, SIZE))
                nc.vector.tensor_tensor(x[:, bass.ds(at.times(SIZE), SIZE), :],
                                        out_banks[:, at.n % 2, :].rearrange("p (k d) -> p k d", k=SIZE),
                                        base[:, at.n % 2, :, :], ALU.add).then_inc(out_added, 1)

            def step(t):
                if here(t, 2):
                    statistics(t.plus(2))
                if gated and here(t, 1):
                    gate(t.plus(1))
                if here(t, 2):
                    normalise(t.plus(2))
                    scale_turned(t.plus(2))
                if here(t, 0):
                    finish(t)

            steps(dve, step)

        @block.gpsimd
        def _(pool):
            for semaphore, value in waits:
                pool.wait_ge(semaphore, value)

            def inverse_deviation(at):
                pool.wait_ge(moments_ready, at.times(SIZE, SIZE))
                if at.n >= 1:
                    pool.wait_ge(rows_ready, at.times(SIZE, 0))
                nc.gpsimd.tensor_tensor(var_eps[:, :], moments[:, :, 1], eps[:, :].to_broadcast([TOKENS, SIZE]),
                                        ALU.add).then_inc(var_ready, 1)
                pool.wait_ge(var_ready, at.times(1, 1))
                nc.gpsimd.tensor_tensor(rstd[:, :], var_eps[:, :], minus_half[:, :].to_broadcast([TOKENS, SIZE]),
                                        ALU.pow).then_inc(rstd_ready, 1)

            def residual(at):
                if at.n >= 2:
                    pool.wait_ge(out_added, at.times(1, -1))
                for k in range(SIZE):
                    row = base[:, at.n % 2, k, :]
                    if add_src:
                        nc.gpsimd.tensor_tensor(row, x[:, at.times(SIZE, k), :], src[:, at.times(SIZE, k), :],
                                                ALU.add).then_inc(base_sum, 1)
                        pool.wait_ge(base_sum, at.times(SIZE, k + 1))
                        nc.gpsimd.tensor_tensor(row, row, bias_out[:, :], ALU.add).then_inc(base_ready, 1)
                    else:
                        nc.gpsimd.tensor_tensor(row, x[:, at.times(SIZE, k), :], bias_out[:, :],
                                                ALU.add).then_inc(base_ready, 1)

            def step(t):
                if here(t, 2):
                    inverse_deviation(t.plus(2))
                if here(t, 1):
                    residual(t.plus(1))

            steps(pool, step)


def kernel(**inputs):
    import numpy as _np
    import concourse.bacc as _bacc
    from concourse import mybir as _mybir
    from concourse.bass_utils import run_bass_kernel_spmd as _run

    nc = _bacc.Bacc("TRN2", target_bir_lowering=False, num_devices=1)
    arrays, aps = {}, {}
    for name in inputs:
        value = _np.ascontiguousarray(inputs[name])
        arrays[f"in_{name}"] = value
        aps[name] = nc.dram_tensor(f"in_{name}", value.shape, _mybir.dt.from_np(value.dtype),
                                   kind="ExternalInput").ap()
    result = nc.dram_tensor("out_x", (BATCHES, TOKENS, DIM), _mybir.dt.float32, kind="ExternalOutput").ap()
    build(nc, aps, result)
    done = _run(nc, [arrays], core_ids=[0])
    return done.results[0]["out_x"]
```

```python
from contextlib import ExitStack

import concourse.bass as bass
from concourse import mybir

FP32 = mybir.dt.float32
ALU = mybir.AluOpType
ACT = mybir.ActivationFunctionType
AX = mybir.AxisListType

BATCHES, TOKENS, DIM = 32, 128, 128
CTX = 96
HEADS = 16
WIDE = 64
NARROW = DIM // HEADS
INNER = HEADS * WIDE
EPS = 1e-5
FF_HIDDEN = 4 * DIM
BANK = 512
START_COUNT = 10
SLOT_HEADS = 8


class At:

    def __init__(self, n, i=None):
        self.n, self.i = n, i

    def plus(self, k):
        return At(self.n + k, self.i)

    def times(self, per, k=0):
        if self.i is None:
            return per * self.n + k
        return self.i * per + (per * self.n + k)

    @property
    def index(self):
        return self.times(1)


class Ring:

    BANKS = 4

    def __init__(self, order, steps, batches, other_orders):
        self.batches = batches
        self.nth, self.fill, self.at_fill = {}, {}, []
        seen = {"act": 0, "dve": 0}
        self.per_step = dict.fromkeys(seen, 0)
        for _, _, engine in order:
            self.per_step[engine] += 1
        self.engine = {name: engine for name, _, engine in order}
        for step in steps:
            for name, lag, engine in other_orders.get(step, order):
                if 0 <= step + lag < batches:
                    seen[engine] += 1
                    self.nth[name, step + lag] = seen[engine]
                    self.fill[name, step + lag] = len(self.at_fill)
                    self.at_fill.append((engine, seen[engine]))

    def count(self, name, at):
        base = self.nth[name, at.n]
        return base if at.i is None else at.i * self.per_step[self.engine[name]] + base

    def bank(self, name, at):
        return self.fill[name, at.n] % self.BANKS

    def before(self, name, at):
        n = self.fill[name, at.n] - self.BANKS
        if n < 0:
            return None
        engine, base = self.at_fill[n]
        return engine, (base if at.i is None else at.i * self.per_step[engine] + base)


def pipeline(engine, step, first, last, steady_first, steady_last, before_loop=lambda: None):
    count = (steady_last - steady_first + 1) // 2 * 2
    for t in range(first, steady_first):
        step(At(t))
    before_loop()
    with engine.Fori(0, count // 2) as turn:
        i = turn * 2
        step(At(steady_first, i))
        step(At(steady_first + 1, i))
    for t in range(steady_first + count, last + 1):
        step(At(t))


def keep_clock(nc, to, ident, count):
    for _ in range(count):
        nc.tensor.matmul(to, ident[:, :], ident[:, :], start=True, stop=True)


def build(nc, a, out):
    ctx = ExitStack()
    with ctx:
        def sb(name, shape):
            return ctx.enter_context(nc.sbuf_tensor(name, shape, FP32))

        def sem(name):
            return ctx.enter_context(nc.semaphore(name))

        x = sb("x", [TOKENS, BATCHES, DIM])
        ctxT = sb("ctxT", [CTX + 1, BATCHES, TOKENS])
        ident = sb("ident", [128, 128])
        ones_row = CTX
        W = {}
        for layer in ("L0a", "L0b", "L2"):
            for w in ("q", "k", "v"):
                W[layer, w] = sb(f"{layer}_w{w}", [DIM, INNER])
            W[layer, "o"] = sb(f"{layer}_wo", [128, INNER // 128, DIM])
        for layer in ("L1", "L3"):
            for w in ("q", "k", "v", "o"):
                W[layer, w] = sb(f"{layer}_w{w}", [128, DIM])
        for w in ("q", "k", "v", "o"):
            W["L3", w + "T"] = sb(f"L3_w{w}T", [128, DIM])
        bq = sb("bq", [128, 1])
        head_mask = sb("head_mask", [128, SLOT_HEADS])
        wp = sb("wp", [DIM, 2 * FF_HIDDEN])
        wf2 = sb("wf2", [128, 4, DIM])
        w1 = sb("w1", [DIM, FF_HIDDEN])
        w2 = sb("w2", [128, 4, DIM])
        bp = sb("bp", [128, 8])
        b1 = sb("b1", [128, 4])
        norm = {n: (sb(f"{n}_g", [DIM, 1]), sb(f"{n}_b", [DIM, 1])) for n in ("ln1", "ln2", "ln3", "L1_ln", "L2_ln")}
        bias = {n: sb(f"bias_{n}", [128, DIM]) for n in ("L0a", "L0b", "L0ff", "L1", "L1ff", "L2", "L3")}
        minus_half = sb("minus_half", [128, 1])
        eps = sb("eps", [128, 1])

        consts_ready = sem("consts_ready")
        mask_ready = sem("mask_ready")
        ctx_bank_full = sem("ctx_bank_full")
        ctx_bank_copied = {"dve": sem("ctx_bank_copied_dve"), "act": sem("ctx_bank_copied_act")}
        w3_bank_full = sem("w3_bank_full")
        early = BATCHES // 4
        groups = ("x_early", "x", "ctx", "ln1", "L0a_qk", "L0a", "L0b", "L0ff", "L1", "L2", "L3")
        loaded = {g: sem(f"loaded_{g}") for g in groups}
        stored = sem("stored")
        loads = dict.fromkeys(loaded, 0)

        def load(queue, group, dst, src):
            loads[group] += 16
            queue.dma_start(dst, src).then_inc(loaded[group], 16)

        def column(v):
            return v.rearrange("(p a) -> p a", a=1)

        x_dram = a["x"].rearrange("b p d -> p b d")
        out_dram = out.rearrange("b p d -> p b d")

        def load_norm(queue, group, norm_name, g, b):
            load(queue, group, norm[norm_name][0][:, :], column(a[g]))
            load(queue, group, norm[norm_name][1][:, :], column(a[b]))

        def load_wide(queue, group, layer, suffix, ctx_rows):
            for w, rows in (("k", ctx_rows), ("q", DIM), ("v", ctx_rows)):
                load(queue, group, W[layer, w][0:rows, :], a[f"{layer[0:2]}_xattn_W{w}{suffix}"])
            load(queue, group, W[layer, "o"][:, :, :],
                 a[f"{layer[0:2]}_xattn_Wo{suffix}"].rearrange("(c p) n -> p c n", p=128))
            load(queue, group, bias[layer][:, :], a[f"{layer[0:2]}_xattn_bo{suffix}"].partition_broadcast(128))

        with nc.Block() as block:
            @block.sync
            def _(sp):
                load(sp, "x_early", x[:, 0:early, :], x_dram[:, 0:early, :])
                load_norm(sp, "ln1", "ln1", "L0_xattn_ln1_g", "L0_xattn_ln1_b")
                for w in ("q", "k"):
                    load(sp, "L0a_qk", W["L0a", w][:, :], a[f"L0_xattn_W{w}1"])

            @block.gpsimd
            def _(pool):
                nc.gpsimd.memset(ident[:, :], 0.0).then_inc(consts_ready, 1)
                pool.wait_ge(consts_ready, 1)
                nc.gpsimd.affine_select(out=ident[:, :], in_=ident[:, :], compare_op=ALU.not_equal, fill=1.0,
                                        base=0, pattern=[[-1, 128]], channel_multiplier=1).then_inc(consts_ready, 1)
                nc.gpsimd.memset(minus_half[:, :], -0.5).then_inc(consts_ready, 1)
                nc.gpsimd.memset(eps[:, :], EPS).then_inc(consts_ready, 1)
                pool.wait_ge(consts_ready, 4)

        def later_loads(sp):
            load(sp, "L0a", W["L0a", "v"][:, :], a["L0_xattn_Wv1"])
            load(sp, "L0a", W["L0a", "o"][:, :, :], a["L0_xattn_Wo1"].rearrange("(c p) n -> p c n", p=128))
            load(sp, "L0a", bias["L0a"][:, :], a["L0_xattn_bo1"].partition_broadcast(128))
            load(sp, "x", x[:, early:, :], x_dram[:, early:, :])
            load(sp, "ctx", ctx_rows[:, :, :], a["ctx_768"].rearrange("b p d -> p b d"))
            for w in ("q", "k", "v", "o"):
                src = a[f"L3_xattn_W{w}"]
                load(sp, "L3", W["L3", w][:, 0:src.shape[1]], src)
            load(sp, "L3", bias["L3"][:, :], a["L3_xattn_bo"].partition_broadcast(128))
            load_norm(sp, "L0b", "ln2", "L0_xattn_ln2_g", "L0_xattn_ln2_b")
            load_wide(sp, "L0b", "L0b", "2", CTX)
            load_norm(sp, "L0ff", "ln3", "L0_xattn_ln3_g", "L0_xattn_ln3_b")
            load(sp, "L0ff", wp[:, :], a["L0_xattn_Wp"])
            load(sp, "L0ff", wf2[:, :, :], a["L0_xattn_Wf2"].rearrange("(c p) n -> p c n", p=128))
            load(sp, "L0ff", bp[:, :], a["L0_xattn_bp"].rearrange("(c p) -> p c", p=128))
            load(sp, "L0ff", bias["L0ff"][:, :], a["L0_xattn_bf2"].partition_broadcast(128))
            load(sp, "L1", bq[:, :], column(a["L1_xattn_bq"]))
            load(sp, "L1", W["L1", "q"][:, :], a["L1_xattn_Wq"])
            for w in ("k", "v"):
                load(sp, "L1", W["L1", w][0:CTX, :], a[f"L1_xattn_W{w}"])
                load(sp, "L1", W["L1", w][ones_row:ones_row + 1, :],
                     a[f"L1_xattn_b{w}"].rearrange("(a n) -> a n", a=1))
            load(sp, "L1", W["L1", "o"][:, :], a["L1_xattn_Wo"])
            load(sp, "L1", bias["L1"][:, :], a["L1_xattn_bo"].partition_broadcast(128))
            load_norm(sp, "L1", "L1_ln", "L1_xattn_ln_g", "L1_xattn_ln_b")
            load(sp, "L1", w1[:, :], a["L1_xattn_W1"])
            load(sp, "L1", w2[:, :, :], a["L1_xattn_W2"].rearrange("(c p) n -> p c n", p=128))
            load(sp, "L1", b1[:, :], a["L1_xattn_b1"].rearrange("(c p) -> p c", p=128))
            load(sp, "L1", bias["L1ff"][:, :], a["L1_xattn_b2"].partition_broadcast(128))
            load_norm(sp, "L2", "L2_ln", "L2_xattn_gamma", "L2_xattn_beta")
            load_wide(sp, "L2", "L2", "", CTX)

        L0A_LATE, X_LATE = 16 * 3, 16
        with nc.sbuf_tensor("ctx_rows", [TOKENS, BATCHES, CTX], FP32) as ctx_rows:
            with nc.allow_non_contiguous_dma(reason="a few hundred bias elements, once"):
                attention(nc, "L0a", x, x, None, W["L0a", "q"], W["L0a", "k"], W["L0a", "v"], W["L0a", "o"],
                          ident, minus_half, eps, bias["L0a"], norm["ln1"], head=WIDE, kv_rows=DIM,
                          scale=WIDE ** -0.5, waits=[(loaded["x_early"], 16), (loaded["ln1"], 16 * 2)],
                          tensor_waits=[(loaded["L0a_qk"], 16 * 2)],
                          late_weights=(loaded["L0a"], L0A_LATE), late_x=(loaded["x"], X_LATE),
                          sync_program=later_loads)

            with ExitStack() as work:
                banks = work.enter_context(nc.psum_tensor("setup_banks", [128, 8, BANK], FP32))
                block = work.enter_context(nc.Block())

                @block.gpsimd
                def _(pool):
                    nc.gpsimd.memset(ctxT[ones_row:ones_row + 1, :, :], 1.0).then_inc(mask_ready, 1)
                    pool.wait_ge(mask_ready, 1)
                    nc.gpsimd.memset(head_mask[:, :], 1.0).then_inc(mask_ready, 1)
                    steps = 2
                    for lo in (0, 64):
                        for base, sign in ((0, 1), (NARROW - 1, -1)):
                            pool.wait_ge(mask_ready, steps)
                            part = head_mask[lo:lo + 64, :]
                            nc.gpsimd.affine_select(out=part, in_=part, compare_op=ALU.is_ge, fill=0.0, base=base,
                                                    pattern=[[-NARROW * sign, SLOT_HEADS]],
                                                    channel_multiplier=sign).then_inc(mask_ready, 1)
                            steps += 1
                    pool.wait_ge(mask_ready, steps)

                @block.tensor
                def _(pe):
                    pe.wait_ge(loaded["ctx"], 16)
                    for n in range(BATCHES // 4):
                        if n >= 4:
                            pe.wait_ge(ctx_bank_copied["act" if n % 2 else "dve"], (n - 4) // 2 + 1)
                        for k in range(4):
                            last = nc.tensor.transpose(banks[0:CTX, 4 + n % 4, 128 * k:128 * k + 128],
                                                       ctx_rows[:, 4 * n + k, :], ident[:, :])
                        last.then_inc(ctx_bank_full, 1)
                    pe.wait_ge(loaded["L3"], 16 * 5)
                    for n, (w, cols) in enumerate((("q", DIM), ("k", CTX), ("v", CTX), ("o", DIM))):
                        nc.tensor.transpose(banks[0:cols, n, 0:DIM], W["L3", w][:, 0:cols],
                                            ident[:, :]).then_inc(w3_bank_full, 1)

                def copy_ctx(n):
                    return (ctxT[0:CTX, 4 * n:4 * n + 4, :],
                            banks[0:CTX, 4 + n % 4, :].rearrange("p (b t) -> p b t", b=4))

                @block.vector
                def _(dve):
                    for n in range(0, BATCHES // 4, 2):
                        dve.wait_ge(ctx_bank_full, n + 1)
                        nc.vector.tensor_copy(*copy_ctx(n)).then_inc(ctx_bank_copied["dve"], 1)
                    for n, (w, rows) in enumerate((("q", DIM), ("k", CTX), ("v", CTX), ("o", DIM))):
                        dve.wait_ge(w3_bank_full, n + 1)
                        nc.vector.tensor_copy(W["L3", w + "T"][0:rows, :], banks[0:rows, n, 0:DIM])

                @block.scalar
                def _(act):
                    for n in range(1, BATCHES // 4, 2):
                        act.wait_ge(ctx_bank_full, n + 1)
                        nc.scalar.activation(*copy_ctx(n), ACT.Copy).then_inc(ctx_bank_copied["act"], 1)

        attention(nc, "L0b", x, x, ctxT, W["L0b", "q"], W["L0b", "k"], W["L0b", "v"], W["L0b", "o"],
                  ident, minus_half, eps, bias["L0b"], norm["ln2"], head=WIDE, kv_rows=CTX, scale=WIDE ** -0.5,
                  waits=[(loaded["L0b"], loads["L0b"])])
        feed_forward(nc, "L0ff", x, x, wp, wf2, bp, bias["L0ff"], norm["ln3"], ident, minus_half, eps, gated=True,
                     waits=[(loaded["L0ff"], loads["L0ff"])])
        with nc.sbuf_tensor("y", [TOKENS, BATCHES, DIM], FP32) as y:
            attention(nc, "L1", x, y, ctxT, W["L1", "q"], W["L1", "k"], W["L1", "v"], W["L1", "o"],
                      ident, minus_half, eps, bias["L1"], None, head=NARROW, kv_rows=CTX + 1, scale=NARROW ** -0.5,
                      waits=[(loaded["L1"], loads["L1"])], q_bias=bq, head_mask=head_mask)
            feed_forward(nc, "L1ff", x, y, w1, w2, b1, bias["L1ff"], norm["L1_ln"], ident, minus_half, eps, gated=False,
                         waits=[(loaded["L1"], loads["L1"])])
        attention(nc, "L2", x, x, ctxT, W["L2", "q"], W["L2", "k"], W["L2", "v"], W["L2", "o"],
                  ident, minus_half, eps, bias["L2"], norm["L2_ln"], head=WIDE, kv_rows=CTX, scale=1.0,
                  out_scale=WIDE ** -0.5, waits=[(loaded["L2"], loads["L2"])])
        attention(nc, "L3", x, x, ctxT, W["L3", "qT"], W["L3", "kT"], W["L3", "vT"], W["L3", "oT"],
                  ident, minus_half, eps, bias["L3"], None, head=NARROW, kv_rows=CTX, scale=NARROW ** -0.5,
                  waits=[(loaded["L3"], loads["L3"])], head_mask=head_mask, store=(out_dram, stored))


def attention(nc, layer, x, dst, ctxT, wq, wk, wv, wo, ident, minus_half, eps, bias_o, norm, *, head, kv_rows,
              scale, waits, tensor_waits=None, q_bias=None, head_mask=None, out_scale=1.0, late_weights=None,
              late_x=None, sync_program=None, store=None):
    wide = head == WIDE
    residual = dst is x
    self_attention = ctxT is None
    if wide:
        order = [("Wo", -1, "dve"), ("T0", 0, "act"), ("T1", 0, "act"), ("q0", 2, "act"), ("k0", 2, "act"),
                 ("PV0", 0, "dve"), ("T2", 0, "act"), ("T3", 0, "act"), ("q1", 2, "act"), ("k1", 2, "act"),
                 ("v0", 1, "act"), ("v1", 1, "act"), ("hT", 3, "dve"), ("PV1", 0, "dve")]
    else:
        order = [("PV0", -1, "dve"), ("hT", 3, "dve"), ("qk", 2, "act"), ("T0", 0, "act"), ("T1", 0, "act"),
                 ("Wo", -1, "dve"), ("T2", 0, "act"), ("T3", 0, "act"), ("v0", 1, "act"), ("iT", 0, "act")]
    first, last = -4, BATCHES
    steady_first, steady_last = 3, BATCHES - 5
    if wide:
        other_orders = {BATCHES - 1: order[1:3] + order[0:1] + order[3:]}
    else:
        other_orders = {t: [order[2], order[1]] + order[3:] for t in (-1, 0)}
    ring = Ring(order, range(first, last + 1), BATCHES, other_orders)
    chunks = INNER // 128
    half_rows = 64
    last_v = "v1" if wide else "v0"
    PROBS_0 = 1 if wide else 2
    GROUP = 4
    QUAD = DIM // 4
    SKEW = QUAD + NARROW

    def here(at, lag):
        return 0 <= at.n + lag < BATCHES

    with ExitStack() as ctx:
        def sb(name, shape):
            return ctx.enter_context(nc.sbuf_tensor(f"{layer}_{name}", shape, FP32))

        def sem(name):
            return ctx.enter_context(nc.semaphore(f"{layer}_{name}"))

        rows_h = sb("rows_h", [TOKENS, DIM])
        hT = sb("hT", [DIM, 2, TOKENS])
        cT = None if self_attention else sb("cT", [kv_rows, 2, TOKENS])
        if wide:
            qT = sb("qT", [128, 2, chunks, TOKENS])
            kT = sb("kT", [128, 2, chunks, TOKENS])
            v = sb("v", [TOKENS, 2, INNER])
            oT = sb("oT", [128, chunks, TOKENS])
        else:
            qT = sb("qT", [128, 2, TOKENS])
            kT = sb("kT", [128, 2, TOKENS])
            k_apart = sb("k_apart", [128, 2, SLOT_HEADS, TOKENS])
            v = sb("v", [TOKENS, 2, 4, 4 * SKEW])
            oT = sb("oT", [128, 1, TOKENS])
            inv_wide = sb("inv_wide", [TOKENS, 2, HEADS, NARROW])
            invT = sb("invT", [128, TOKENS])
        probs = sb("probs", [TOKENS, 1 + PROBS_0, SLOT_HEADS, TOKENS])
        probsT = sb("probsT", [TOKENS, HEADS, TOKENS])
        x_bias = sb("x_bias", [TOKENS, 2, DIM]) if residual else None
        stats = sb("stats", [TOKENS, 2, 6])
        wait_carrier = sb("wait_carrier", [TOKENS, 1])
        table_loader = sb("table_loader", [TOKENS, 1])
        moments = sb("moments", [TOKENS, 2, 2])
        var_eps = sb("var_eps", [TOKENS, 2, 1])
        rstd = sb("rstd", [TOKENS, 2, 1])
        row_max = sb("row_max", [TOKENS, 2, SLOT_HEADS])
        neg_max = sb("neg_max", [TOKENS, SLOT_HEADS])
        sums = sb("sums", [TOKENS, 2, 2, GROUP])
        inv_sum = sb("inv_sum", [TOKENS, 2, 2, GROUP])
        scores = ctx.enter_context(nc.psum_tensor(f"{layer}_scores", [TOKENS, 2, 2, GROUP, TOKENS], FP32))
        ring_banks = ctx.enter_context(nc.psum_tensor(f"{layer}_ring", [128, Ring.BANKS, BANK], FP32))

        filled = {"act": sem("ring_filled_act"), "dve": sem("ring_filled_dve")}
        emptied = {"act": sem("ring_emptied_act"), "dve": sem("ring_emptied_dve")}
        if norm is not None:
            stats_ready, moments_ready = sem("stats_ready"), sem("moments_ready")
            var_ready, rstd_ready = sem("var_ready"), sem("rstd_ready")
        rows_h_ready = sem("rows_h_ready")
        if not self_attention:
            cT_ready = sem("cT_ready")
        if residual:
            x_bias_ready = sem("x_bias_ready")
        scores_full = [sem("scores_full_0"), sem("scores_full_1")]
        max_ready = [sem("max_ready_0"), sem("max_ready_1")]
        neg_max_ready = sem("neg_max_ready")
        shifted = sem("shifted")
        exp_ready = [sem("exp_ready_0"), sem("exp_ready_1")]
        sum_ready = sem("sum_ready")
        inverted = [sem("inverted_0"), sem("inverted_1")]
        if wide:
            divided = sem("divided")
        else:
            v_cleared = sem("v_cleared")
            keys_apart = sem("keys_apart")
            inv_wide_ready = sem("inv_wide_ready")
        block = ctx.enter_context(nc.Block())

        def slot_probs(at, s):
            return probs[:, PROBS_0 if s == 1 else at.n % PROBS_0, :, :]

        def bank(name, at):
            return ring_banks[:, ring.bank(name, at), :]

        def await_filled(engine, name, at):
            engine.wait_ge(filled[ring.engine[name]], ring.count(name, at))

        def await_emptied(engine, name, at):
            engine.wait_ge(emptied[ring.engine[name]], ring.count(name, at))

        def steps(engine, step):
            def before_loop():
                if late_x:
                    engine.wait_ge(*late_x)
            pipeline(engine, step, first, last, steady_first, steady_last, before_loop)

        if sync_program is not None:
            block.sync(sync_program)

        @block.tensor
        def _(pe):
            idle_bank = scores[:, 0, 0, 0, :]
            keep_clock(nc, idle_bank, ident, START_COUNT)
            for semaphore, value in tensor_waits or waits:
                pe.wait_ge(semaphore, value)

            def start_fill(name, at):
                before = ring.before(name, at)
                if before:
                    pe.wait_ge(emptied[before[0]], before[1])
                return bank(name, at)

            def filled_by(instruction, name):
                instruction.then_inc(filled[ring.engine[name]], 1)

            def score(at, s):
                p = at.n % 2
                if wide:
                    await_emptied(pe, f"q{s}", at)
                    await_emptied(pe, f"k{s}", at)
                else:
                    pe.wait_ge(keys_apart, at.times(1, 1))
                if at.n >= 1 and s == 1:
                    pe.wait_ge(shifted, at.times(1, 0))
                for i in range(GROUP if wide else 1):
                    for r in range(2):
                        if at.n >= 1 and s == 0 and i == 0:
                            pe.wait_ge(exp_ready[0], at.times(2, r - 1))
                        part = slice(half_rows * r, half_rows * (r + 1))
                        if wide:
                            c = GROUP * s + i
                            to, q, k = scores[:, s, r, i, :], qT[part, p, c, :], kT[part, p, c, :]
                        else:
                            to, q = scores[:, s, r, :, :], qT[part, p, :]
                            k = k_apart[part, p, GROUP * s:GROUP * (s + 1), :]
                        last = nc.tensor.matmul(to, q, k, start=True, stop=True, tile_position=(half_rows * r, 0))
                last.then_inc(scores_full[s], 1)

            def transpose_probs(at, n):
                s, r = divmod(n, 2)
                if r == 0:
                    if wide:
                        pe.wait_ge(divided, at.times(2, s + 1))
                    else:
                        pe.wait_ge(exp_ready[s], at.times(2, 2) if s == 0 else at.times(1, 1))
                to = start_fill(f"T{n}", at)
                for i in range(GROUP):
                    last = nc.tensor.transpose(to[:, TOKENS * i:TOKENS * (i + 1)],
                                               slot_probs(at, s)[:, GROUP * r + i, :], ident[:, :])
                filled_by(last, f"T{n}")

            def project_T(name, at, w, src, src_rows, n):
                to = start_fill(name, at)
                for c in range(4):
                    last = nc.tensor.matmul(to[:, TOKENS * c:TOKENS * (c + 1)],
                                            w[0:src_rows, BANK * n + 128 * c:BANK * n + 128 * (c + 1)],
                                            src, start=True, stop=True)
                filled_by(last, name)

            def await_kv_source(at):
                if not self_attention:
                    pe.wait_ge(cT_ready, at.times(1, 1))

            def kv_source(at):
                return (hT if self_attention else cT)[0:kv_rows, at.n % 2, :]

            def queries_keys(at, n):
                if n == 0:
                    await_emptied(pe, "hT", at)
                    await_kv_source(at)
                if wide:
                    project_T(f"q{n}", at, wq, hT[:, at.n % 2, :], DIM, n)
                    project_T(f"k{n}", at, wk, kv_source(at), kv_rows, n)
                else:
                    to = start_fill("qk", at)
                    nc.tensor.matmul(to[:, 0:TOKENS], wq[:, :], hT[:, at.n % 2, :], start=True, stop=True)
                    filled_by(nc.tensor.matmul(to[:, TOKENS:2 * TOKENS], wk[0:kv_rows, :], kv_source(at),
                                               start=True, stop=True), "qk")

            def values(at, n):
                if late_weights and at.n == 0 and n == 0:
                    pe.wait_ge(*late_weights)
                to = start_fill(f"v{n}", at)
                cols = BANK if wide else DIM
                filled_by(nc.tensor.matmul(to[:, 0:cols], kv_source(at), wv[0:kv_rows, cols * n:cols * (n + 1)],
                                           start=True, stop=True), f"v{n}")

            def weigh_wide(at, s):
                if s == 0:
                    await_emptied(pe, last_v, at)
                await_emptied(pe, f"T{2 * s + 1}", at)
                to = start_fill(f"PV{s}", at)
                for i in range(GROUP):
                    for r in range(2):
                        h = 2 * (GROUP * s + i) + r
                        last = nc.tensor.matmul(to[WIDE * r:WIDE * (r + 1), TOKENS * i:TOKENS * (i + 1)],
                                                v[:, at.n % 2, WIDE * h:WIDE * (h + 1)],
                                                probsT[:, SLOT_HEADS * s + GROUP * r + i, :],
                                                start=True, stop=True, tile_position=(0, WIDE * r))
                filled_by(last, f"PV{s}")

            def weigh_narrow(at):
                await_emptied(pe, last_v, at)
                await_emptied(pe, "T3", at)
                to = start_fill("PV0", at)
                for j in range(4):
                    for g in range(4):
                        r, s = divmod(g, 2)
                        last = nc.tensor.matmul(to[QUAD * g:QUAD * (g + 1), 0:TOKENS],
                                                v[:, at.n % 2, g, QUAD * j:QUAD * (j + 1)],
                                                probsT[:, SLOT_HEADS * s + GROUP * r + j, :],
                                                start=j == 0, stop=j == 3, tile_position=(0, QUAD * g))
                filled_by(last, "PV0")

            def transpose_inverses(at):
                pe.wait_ge(inv_wide_ready, at.times(1, 1))
                filled_by(nc.tensor.transpose(start_fill("iT", at)[:, 0:TOKENS],
                                              inv_wide[:, at.n % 2, :, :].rearrange("p h d -> p (h d)"),
                                              ident[:, :]), "iT")

            def transpose_h(at):
                pe.wait_ge(rows_h_ready, at.times(1, 1))
                filled_by(nc.tensor.transpose(start_fill("hT", at)[:, 0:TOKENS], rows_h[:, :], ident[:, :]), "hT")

            def project_out(at):
                await_emptied(pe, "PV0", at)
                to = start_fill("Wo", at)
                pieces = chunks if wide else 1
                for c in range(pieces):
                    if c == GROUP:
                        await_emptied(pe, "PV1", at)
                    w = wo[:, c, :] if wide else wo[:, :]
                    last = nc.tensor.matmul(to[:, 0:DIM], oT[:, c, :], w, start=c == 0, stop=c == pieces - 1)
                filled_by(last, "Wo")

            def wide_step(t):
                before_last = here(t, 1) and not here(t, 2)
                if here(t, 1):
                    score(t.plus(1), 0)
                if before_last:
                    score(t.plus(1), 1)
                if here(t, -1) and here(t, 1):
                    project_out(t.plus(-1))
                if here(t, 0):
                    transpose_probs(t, 0)
                    transpose_probs(t, 1)
                if here(t, -1) and not here(t, 1):
                    project_out(t.plus(-1))
                if here(t, 2):
                    queries_keys(t.plus(2), 0)
                if here(t, 0):
                    weigh_wide(t, 0)
                if here(t, 1) and not before_last:
                    score(t.plus(1), 1)
                if here(t, 0):
                    transpose_probs(t, 2)
                    transpose_probs(t, 3)
                if here(t, 2):
                    queries_keys(t.plus(2), 1)
                if here(t, 1):
                    values(t.plus(1), 0)
                    values(t.plus(1), 1)
                if here(t, 3):
                    transpose_h(t.plus(3))
                if here(t, 0):
                    weigh_wide(t, 1)

            def narrow_step(t):
                projections_first = t.n in (-1, 0)
                if here(t, 1) and not projections_first:
                    score(t.plus(1), 0)
                if here(t, -1):
                    weigh_narrow(t.plus(-1))
                if projections_first:
                    queries_keys(t.plus(2), 0)
                    if t.n == -1:
                        keep_clock(nc, idle_bank, ident, START_COUNT)
                    score(t.plus(1), 0)
                if here(t, 3):
                    transpose_h(t.plus(3))
                if here(t, 2) and not projections_first:
                    queries_keys(t.plus(2), 0)
                if here(t, 0):
                    transpose_probs(t, 0)
                    transpose_probs(t, 1)
                if here(t, -1):
                    project_out(t.plus(-1))
                if here(t, 1):
                    score(t.plus(1), 1)
                if here(t, 0):
                    transpose_probs(t, 2)
                    transpose_probs(t, 3)
                if here(t, 1):
                    values(t.plus(1), 0)
                if here(t, 0):
                    transpose_inverses(t)

            steps(pe, wide_step if wide else narrow_step)

        @block.scalar
        def _(act):
            nc.scalar.activation(table_loader[:, :], eps[:, :], ACT.Exp)

            def copied(to, src):
                nc.scalar.activation(to, src, ACT.Copy).then_inc(emptied["act"], 1)

            def exponentiate_0(at, r):
                if r == 0:
                    act.wait_ge(neg_max_ready, at.times(1, 1))
                    if at.n >= 1:
                        act.wait_ge(inverted[0], at.times(1, 0))
                for i in range(GROUP):
                    n = GROUP * r + i
                    done = nc.scalar.activation(slot_probs(at, 0)[:, n, :], scores[:, 0, r, i, :], ACT.Exp, scale=scale,
                                                bias=neg_max[:, n:n + 1], accum_out=sums[:, r, 0, i:i + 1])
                done.then_inc(exp_ready[0], 1)

            def exponentiate_1(at):
                act.wait_ge(shifted, at.times(1, 1))
                nc.scalar.activation(slot_probs(at, 1), slot_probs(at, 1), ACT.Exp,
                                     scale=scale).then_inc(exp_ready[1], 1)

            def projections(at, n):
                p = at.n % 2
                if wide:
                    for name, to in ((f"q{n}", qT), (f"k{n}", kT)):
                        await_filled(act, name, at)
                        copied(to[:, p, 4 * n:4 * n + 4, :].rearrange("p c t -> p (c t)"), bank(name, at))
                else:
                    await_filled(act, "qk", at)
                    if at.n >= 2:
                        act.wait_ge(keys_apart, at.times(1, -1))
                    src = bank("qk", at)
                    if q_bias is None:
                        nc.scalar.activation(qT[:, p, :], src[:, 0:TOKENS], ACT.Copy)
                    else:
                        nc.scalar.activation(qT[:, p, :], src[:, 0:TOKENS], ACT.Identity, bias=q_bias[:, :])
                    copied(kT[:, p, :], src[:, TOKENS:2 * TOKENS])

            def values(at):
                if wide:
                    for n in range(2):
                        await_filled(act, f"v{n}", at)
                        copied(v[:, at.n % 2, BANK * n:BANK * (n + 1)], bank(f"v{n}", at))
                else:
                    if at.n == 0:
                        act.wait_ge(v_cleared, 1)
                    await_filled(act, "v0", at)
                    copied(v[:, at.n % 2, :, :].rearrange("p g (j k) -> p g j k", k=SKEW)[:, :, :, 0:NARROW],
                           bank("v0", at)[:, 0:DIM].rearrange("p (g j d) -> p g j d", j=4, d=NARROW))

            def turned_probs(at, n):
                await_filled(act, f"T{n}", at)
                copied(probsT[:, GROUP * n:GROUP * (n + 1), :].rearrange("p h t -> p (h t)"), bank(f"T{n}", at))

            def wide_step(t):
                before_last = here(t, 1) and not here(t, 2)
                if here(t, 0):
                    turned_probs(t, 0)
                    turned_probs(t, 1)
                if here(t, 2):
                    projections(t.plus(2), 0)
                if here(t, 1):
                    exponentiate_0(t.plus(1), 0)
                if before_last:
                    exponentiate_0(t.plus(1), 1)
                if here(t, 0):
                    turned_probs(t, 2)
                    turned_probs(t, 3)
                if here(t, 1) and not before_last:
                    exponentiate_0(t.plus(1), 1)
                if here(t, 2):
                    projections(t.plus(2), 1)
                if before_last:
                    exponentiate_1(t.plus(1))
                if here(t, 1):
                    values(t.plus(1))
                if here(t, 1) and not before_last:
                    exponentiate_1(t.plus(1))

            def narrow_step(t):
                if here(t, 2):
                    projections(t.plus(2), 0)
                if here(t, 1):
                    exponentiate_0(t.plus(1), 0)
                if here(t, 0):
                    turned_probs(t, 0)
                    turned_probs(t, 1)
                if here(t, 1):
                    exponentiate_0(t.plus(1), 1)
                if here(t, 0):
                    turned_probs(t, 2)
                    turned_probs(t, 3)
                if here(t, 1):
                    values(t.plus(1))
                if here(t, 0):
                    await_filled(act, "iT", t)
                    copied(invT[:, :], bank("iT", t)[:, 0:TOKENS])
                if here(t, 1):
                    exponentiate_1(t.plus(1))

            steps(act, wide_step if wide else narrow_step)

        @block.vector
        def _(dve):
            for semaphore, value in waits:
                dve.wait_ge(semaphore, value)

            def statistics(at):
                p = at.n % 2
                nc.vector.bn_stats(stats[:, p, :], x[:, at.index, :]).then_inc(stats_ready, 1)
                dve.wait_ge(stats_ready, at.times(1, 1))
                nc.vector.memset(wait_carrier[:, :], 0.0)
                nc.vector.bn_aggr(moments[:, p, :], stats[:, p, :]).then_inc(moments_ready, 1)

            def normalise(at):
                p = at.n % 2
                dve.wait_ge(moments_ready, at.times(1, 1))
                dve.wait_ge(rstd_ready, at.times(1, 1))
                if at.n >= 1:
                    await_filled(dve, "hT", at.plus(-1))
                nc.vector.tensor_scalar(rows_h[:, :], x[:, at.index, :], moments[:, p, 0:1], rstd[:, p, :],
                                        ALU.subtract, ALU.mult).then_inc(rows_h_ready, 1)

            def slot(s):
                return scores[:, s, :, :, :].rearrange("p r i k -> p (r i) k")

            def row_maxima(at, s):
                dve.wait_ge(scores_full[s], at.times(1, 1))
                nc.vector.tensor_reduce(row_max[:, s, :], slot(s), AX.X, ALU.max).then_inc(max_ready[s], 1)
                dve.wait_ge(max_ready[s], at.times(1, 1))

            def negate_maxima(at):
                if at.n >= 1:
                    dve.wait_ge(exp_ready[0], at.times(2, 0))
                nc.vector.tensor_scalar(neg_max[:, :], row_max[:, 0, :], -scale, None,
                                        ALU.mult).then_inc(neg_max_ready, 1)

            def subtract_maxima(at):
                if at.n >= 1:
                    await_filled(dve, "T3", at.plus(-1))
                nc.vector.tensor_tensor(slot_probs(at, 1), slot(1),
                                        row_max[:, 1, :].unsqueeze(2).to_broadcast([TOKENS, SLOT_HEADS, TOKENS]),
                                        ALU.subtract).then_inc(shifted, 1)

            def add_up(at):
                dve.wait_ge(exp_ready[1], at.times(1, 1))
                nc.vector.tensor_reduce(sums[:, :, 1, :], slot_probs(at, 1).rearrange("p (r i) k -> p r i k", r=2),
                                        AX.X, ALU.add).then_inc(sum_ready, 1)

            def invert(at, s):
                if s == 0:
                    dve.wait_ge(exp_ready[0], at.times(2, 2))
                else:
                    dve.wait_ge(sum_ready, at.times(1, 1))
                if wide and at.n >= 1:
                    dve.wait_ge(divided, at.times(2, s - 1))
                nc.vector.reciprocal(inv_sum[:, :, s, :], sums[:, :, s, :]).then_inc(inverted[s], 1)

            def repeat_inverses(at):
                dve.wait_ge(inverted[1], at.times(1, 1))
                nc.vector.tensor_copy(inv_wide[:, at.n % 2, :, :],
                                      inv_sum[:, :, :, :].rearrange("p r s i -> p (r s i)").unsqueeze(2)
                                      .to_broadcast([TOKENS, HEADS, NARROW])).then_inc(inv_wide_ready, 1)

            def weighted_wide(at, s):
                await_filled(dve, f"PV{s}", at)
                nc.vector.tensor_copy(oT[:, GROUP * s:GROUP * (s + 1), :].rearrange("p c t -> p (c t)"),
                                      bank(f"PV{s}", at)).then_inc(emptied["dve"], 1)

            def weighted_narrow(at):
                await_emptied(dve, "iT", at)
                await_filled(dve, "PV0", at)
                nc.vector.tensor_tensor(oT[:, 0, :], bank("PV0", at)[:, 0:TOKENS], invT[:, :],
                                        ALU.mult).then_inc(emptied["dve"], 1)

            def turned_h(at):
                await_filled(dve, "hT", at)
                src = bank("hT", at)[:, 0:TOKENS]
                if norm is None:
                    nc.vector.tensor_copy(hT[:, at.n % 2, :], src).then_inc(emptied["dve"], 1)
                else:
                    nc.vector.tensor_scalar(hT[:, at.n % 2, :], src, norm[0][:, :], norm[1][:, :],
                                            ALU.mult, ALU.add).then_inc(emptied["dve"], 1)

            def finish(at):
                await_filled(dve, "Wo", at)
                if residual:
                    dve.wait_ge(x_bias_ready, at.times(1, 1))
                    plus = x_bias[:, at.n % 2, :]
                else:
                    plus = bias_o[:, :]
                src = bank("Wo", at)[:, 0:DIM]
                if out_scale == 1.0:
                    done = nc.vector.tensor_tensor(dst[:, at.index, :], src, plus, ALU.add)
                else:
                    done = nc.vector.scalar_tensor_tensor(dst[:, at.index, :], src, out_scale, plus,
                                                          ALU.mult, ALU.add)
                done.then_inc(emptied["dve"], 1)

            def wide_step(t):
                before_last = here(t, 1) and not here(t, 2)
                invert_early = before_last or t.n == -1
                if here(t, 1):
                    row_maxima(t.plus(1), 0)
                    negate_maxima(t.plus(1))
                if here(t, -1) and here(t, 1):
                    finish(t.plus(-1))
                if here(t, 0):
                    add_up(t)
                    invert(t, 1)
                if here(t, -1) and not here(t, 1):
                    finish(t.plus(-1))
                if here(t, 4):
                    statistics(t.plus(4))
                if before_last:
                    row_maxima(t.plus(1), 1)
                if here(t, 0):
                    weighted_wide(t, 0)
                if here(t, 3):
                    normalise(t.plus(3))
                if here(t, 1) and not before_last:
                    row_maxima(t.plus(1), 1)
                if invert_early:
                    invert(t.plus(1), 0)
                if here(t, 1):
                    subtract_maxima(t.plus(1))
                if here(t, 3):
                    turned_h(t.plus(3))
                if here(t, 0):
                    weighted_wide(t, 1)
                if here(t, 1) and not invert_early:
                    invert(t.plus(1), 0)

            def narrow_step(t):
                if here(t, 1):
                    row_maxima(t.plus(1), 0)
                    negate_maxima(t.plus(1))
                if here(t, -1):
                    weighted_narrow(t.plus(-1))
                if here(t, 3):
                    turned_h(t.plus(3))
                if t.n == -2:
                    nc.vector.memset(v[:, :, :, :], 0.0).then_inc(v_cleared, 1)
                if here(t, 0):
                    add_up(t)
                    invert(t, 1)
                    repeat_inverses(t)
                if here(t, -1):
                    finish(t.plus(-1))
                if here(t, 1):
                    row_maxima(t.plus(1), 1)
                    subtract_maxima(t.plus(1))
                    invert(t.plus(1), 0)

            steps(dve, wide_step if wide else narrow_step)

        @block.gpsimd
        def _(pool):
            for semaphore, value in waits:
                pool.wait_ge(semaphore, value)

            def inverse_deviation(at):
                p = at.n % 2
                pool.wait_ge(moments_ready, at.times(1, 1))
                if at.n >= 2:
                    pool.wait_ge(rows_h_ready, at.times(1, -1))
                nc.gpsimd.tensor_tensor(var_eps[:, p, :], moments[:, p, 1:2], eps[:, :], ALU.add).then_inc(var_ready, 1)
                pool.wait_ge(var_ready, at.times(1, 1))
                nc.gpsimd.tensor_tensor(rstd[:, p, :], var_eps[:, p, :], minus_half[:, :],
                                        ALU.pow).then_inc(rstd_ready, 1)

            def copy_rows(at):
                if at.n >= 1:
                    await_filled(pool, "hT", at.plus(-1))
                nc.gpsimd.tensor_copy(rows_h[:, :], x[:, at.index, :]).then_inc(rows_h_ready, 1)

            def add_bias(at):
                if late_weights and at.n == 0:
                    pool.wait_ge(*late_weights)
                if at.n >= 2:
                    await_emptied(pool, "Wo", at.plus(-2))
                nc.gpsimd.tensor_tensor(x_bias[:, at.n % 2, :], x[:, at.index, :], bias_o[:, :],
                                        ALU.add).then_inc(x_bias_ready, 1)

            def stage_context(at):
                if at.n >= 2:
                    await_filled(pool, last_v, at.plus(-2))
                nc.gpsimd.tensor_copy(cT[0:kv_rows, at.n % 2, :],
                                      ctxT[0:kv_rows, at.index, :]).then_inc(cT_ready, 1)

            def set_keys_apart(at):
                p = at.n % 2
                await_emptied(pool, "qk", at)
                nc.gpsimd.tensor_tensor(k_apart[:, p, :, :],
                                        kT[:, p, :].unsqueeze(1).to_broadcast([128, SLOT_HEADS, TOKENS]),
                                        head_mask[:, :].unsqueeze(2).to_broadcast([128, SLOT_HEADS, TOKENS]),
                                        ALU.mult).then_inc(keys_apart, 1)

            def divide(at, s):
                pool.wait_ge(inverted[s], at.times(1, 1))
                to = slot_probs(at, s).rearrange("p (r i) k -> p r i k", r=2)
                nc.gpsimd.tensor_tensor(to, to, inv_sum[:, :, s, :].unsqueeze(3)
                                        .to_broadcast([TOKENS, 2, GROUP, TOKENS]), ALU.mult).then_inc(divided, 1)

            def step(t):
                if wide and here(t, 0):
                    divide(t, 1)
                if norm is not None and here(t, 4):
                    inverse_deviation(t.plus(4))
                if norm is None and here(t, 3):
                    copy_rows(t.plus(3))
                if not self_attention and here(t, 3) and not here(t, 1):
                    stage_context(t.plus(3))
                if not wide and here(t, 2):
                    set_keys_apart(t.plus(2))
                if residual and here(t, 1):
                    add_bias(t.plus(1))
                if wide and t.n == -1:
                    divide(t.plus(1), 0)
                if not self_attention and here(t, 3) and here(t, 1):
                    stage_context(t.plus(3))
                if wide and here(t, 1) and t.n != -1:
                    divide(t.plus(1), 0)

            steps(pool, step)

        if store is not None:
            @block.sync
            def _(sp):
                out_dram, stored = store
                for b in range(BATCHES):
                    await_emptied(sp, "Wo", At(b))
                    sp.dma_start(out_dram[:, b, :], dst[:, b, :]).then_inc(stored, 16)
                sp.wait_ge(stored, 16 * BATCHES)


def feed_forward(nc, layer, x, src, w_in, w_out, b_in, bias_out, norm, ident, minus_half, eps, *, gated, waits):
    SIZE = 2
    GROUPS = BATCHES // SIZE
    CHUNKS = FF_HIDDEN // 128
    add_src = src is not x
    stats_first = (-2, -1) if gated else (-2,)

    def here(at, lag):
        return 0 <= at.n + lag < GROUPS

    with ExitStack() as ctx:
        def sb(name, shape):
            return ctx.enter_context(nc.sbuf_tensor(f"{layer}_{name}", shape, FP32))

        def sem(name):
            return ctx.enter_context(nc.semaphore(f"{layer}_{name}"))

        stats = sb("stats", [TOKENS, 2, SIZE, 6])
        wait_carrier = sb("wait_carrier", [TOKENS, 1])
        table_loader = sb("table_loader", [TOKENS, 1])
        moments = sb("moments", [TOKENS, 2, SIZE, 2])
        var_eps = sb("var_eps", [TOKENS, 2, SIZE])
        rstd = sb("rstd", [TOKENS, 2, SIZE])
        rows_h = sb("rows_h", [TOKENS, SIZE, DIM])
        hT = sb("hT", [DIM, 2, SIZE * TOKENS])
        gelu = sb("gelu", [128, 2, SIZE * TOKENS]) if gated else None
        hidden = sb("hidden", [128, 2, CHUNKS, SIZE * TOKENS])
        base = sb("base", [TOKENS, 2, SIZE, DIM])
        in_banks = ctx.enter_context(nc.psum_tensor(f"{layer}_in", [128, 4, BANK], FP32))
        out_banks = ctx.enter_context(nc.psum_tensor(f"{layer}_out", [128, 2, BANK], FP32))
        turn_banks = ctx.enter_context(nc.psum_tensor(f"{layer}_turn", [128, 2, BANK], FP32))

        stats_ready = sem("stats_ready")
        moments_ready = sem("moments_ready")
        var_ready = sem("var_ready")
        rstd_ready = sem("rstd_ready")
        rows_ready = sem("rows_ready")
        turned = sem("turned")
        hT_ready = sem("hT_ready")
        gate_full = sem("gate_full")
        if gated:
            value_full, gelu_ready = sem("value_full"), sem("gelu_ready")
        hidden_ready = sem("hidden_ready")
        out_full = sem("out_full")
        out_added = sem("out_added")
        if add_src:
            base_sum = sem("base_sum")
        base_ready = sem("base_ready")
        block = ctx.enter_context(nc.Block())

        def steps(engine, step):
            pipeline(engine, step, -3, GROUPS - 1, 2, GROUPS - 4)

        def gate_bank(c):
            return in_banks[:, c % 2 if gated else c, 0:SIZE * TOKENS]

        def value_bank(c):
            return in_banks[:, 2 + c % 2, 0:SIZE * TOKENS]

        @block.tensor
        def _(pe):
            keep_clock(nc, in_banks[:, 0, 0:128], ident, START_COUNT)
            for semaphore, value in waits:
                pe.wait_ge(semaphore, value)

            def transpose_rows(at):
                pe.wait_ge(rows_ready, at.times(SIZE, SIZE))
                if at.n >= 2:
                    pe.wait_ge(hT_ready, at.times(1, -1))
                for k in range(SIZE):
                    last = nc.tensor.transpose(turn_banks[:, at.n % 2, 128 * k:128 * (k + 1)], rows_h[:, k, :],
                                               ident[:, :])
                last.then_inc(turned, 1)

            def expand(at):
                pe.wait_ge(hT_ready, at.times(1, 1))
                for c in range(CHUNKS):
                    if gated:
                        before = at.times(CHUNKS, c - 1)
                        if at.n > 0 or c >= 2:
                            pe.wait_ge(gelu_ready, before)
                    elif at.n > 0:
                        pe.wait_ge(hidden_ready, at.times(CHUNKS, c - 3))
                    gate_col = FF_HIDDEN + 128 * c if gated else 128 * c
                    nc.tensor.matmul(gate_bank(c), w_in[:, gate_col:gate_col + 128], hT[:, at.n % 2, :],
                                     start=True, stop=True).then_inc(gate_full, 1)
                    if gated:
                        if at.n > 0 or c >= 2:
                            pe.wait_ge(hidden_ready, before)
                        nc.tensor.matmul(value_bank(c), w_in[:, 128 * c:128 * c + 128],
                                         hT[:, at.n % 2, :], start=True, stop=True).then_inc(value_full, 1)

            def contract(at):
                pe.wait_ge(hidden_ready, at.times(CHUNKS, CHUNKS))
                if at.n >= 2:
                    pe.wait_ge(out_added, at.times(1, -1))
                for k in range(SIZE):
                    for c in range(CHUNKS):
                        last = nc.tensor.matmul(out_banks[:, at.n % 2, 128 * k:128 * (k + 1)],
                                                hidden[:, at.n % 2, c, 128 * k:128 * (k + 1)], w_out[:, c, :],
                                                start=c == 0, stop=c == CHUNKS - 1)
                last.then_inc(out_full, 1)

            def step(t):
                if t.n == -1:
                    transpose_rows(t.plus(2))
                if here(t, 1):
                    expand(t.plus(1))
                if here(t, 2) and t.n != -1:
                    transpose_rows(t.plus(2))
                if here(t, 0):
                    contract(t)

            steps(pe, step)

        @block.scalar
        def _(act):
            nc.scalar.activation(table_loader[:, :], eps[:, :], ACT.Gelu)
            for semaphore, value in waits:
                act.wait_ge(semaphore, value)

            def activate(at):
                for c in range(CHUNKS):
                    act.wait_ge(gate_full, at.times(CHUNKS, c + 1))
                    if gated:
                        if at.n > 0 or c >= 2:
                            act.wait_ge(hidden_ready, at.times(CHUNKS, c - 1))
                        nc.scalar.activation(gelu[:, c % 2, :], gate_bank(c), ACT.Gelu,
                                             bias=b_in[:, CHUNKS + c:CHUNKS + c + 1]).then_inc(gelu_ready, 1)
                    else:
                        if at.n >= 2:
                            act.wait_ge(out_full, at.times(1, -1))
                        nc.scalar.activation(hidden[:, at.n % 2, c, :], gate_bank(c), ACT.Gelu,
                                             bias=b_in[:, c:c + 1]).then_inc(hidden_ready, 1)

            def step(t):
                if here(t, 1):
                    activate(t.plus(1))

            steps(act, step)

        @block.vector
        def _(dve):
            for semaphore, value in waits:
                dve.wait_ge(semaphore, value)

            def statistics(at):
                for k in range(SIZE):
                    if k == 0 and at.n >= 2:
                        dve.wait_ge(rstd_ready, at.times(1, -1))
                    nc.vector.bn_stats(stats[:, at.n % 2, k, :], src[:, at.times(SIZE, k), :]).then_inc(stats_ready, 1)
                for k in range(SIZE):
                    if k == 0:
                        dve.wait_ge(stats_ready, at.times(SIZE, SIZE))
                        nc.vector.memset(wait_carrier[:, :], 0.0)
                    nc.vector.bn_aggr(moments[:, at.n % 2, k, :], stats[:, at.n % 2, k, :]).then_inc(moments_ready, 1)

            def normalise(at):
                dve.wait_ge(moments_ready, at.times(SIZE, SIZE))
                dve.wait_ge(rstd_ready, at.times(1, 1))
                if at.n >= 1:
                    dve.wait_ge(turned, at.times(1, 0))
                for k in range(SIZE):
                    nc.vector.tensor_scalar(rows_h[:, k, :], src[:, at.times(SIZE, k), :],
                                            moments[:, at.n % 2, k, 0:1], rstd[:, at.n % 2, k:k + 1],
                                            ALU.subtract, ALU.mult).then_inc(rows_ready, 1)

            def scale_turned(at):
                dve.wait_ge(turned, at.times(1, 1))
                nc.vector.tensor_scalar(hT[:, at.n % 2, :], turn_banks[:, at.n % 2, 0:SIZE * TOKENS],
                                        norm[0][:, :], norm[1][:, :],
                                        ALU.mult, ALU.add).then_inc(hT_ready, 1)

            def gate(at):
                for c in range(CHUNKS):
                    dve.wait_ge(value_full, at.times(CHUNKS, c + 1))
                    dve.wait_ge(gelu_ready, at.times(CHUNKS, c + 1))
                    nc.vector.scalar_tensor_tensor(hidden[:, at.n % 2, c, :], value_bank(c),
                                                   b_in[:, c:c + 1], gelu[:, c % 2, :], ALU.add,
                                                   ALU.mult).then_inc(hidden_ready, 1)

            def finish(at):
                dve.wait_ge(out_full, at.times(1, 1))
                dve.wait_ge(base_ready, at.times(SIZE, SIZE))
                nc.vector.tensor_tensor(x[:, bass.ds(at.times(SIZE), SIZE), :],
                                        out_banks[:, at.n % 2, 0:SIZE * DIM].rearrange("p (k d) -> p k d", k=SIZE),
                                        base[:, at.n % 2, :, :], ALU.add).then_inc(out_added, 1)

            def step(t):
                if t.n in stats_first:
                    statistics(t.plus(3))
                if here(t, 2):
                    normalise(t.plus(2))
                if t.n == -1:
                    scale_turned(t.plus(2))
                if gated and here(t, 1):
                    gate(t.plus(1))
                if here(t, 2) and t.n != -1:
                    scale_turned(t.plus(2))
                if here(t, 3) and t.n not in stats_first:
                    statistics(t.plus(3))
                if here(t, 0):
                    finish(t)

            steps(dve, step)

        @block.gpsimd
        def _(pool):
            for semaphore, value in waits:
                pool.wait_ge(semaphore, value)

            def inverse_deviation(at):
                pool.wait_ge(moments_ready, at.times(SIZE, SIZE))
                p = at.n % 2
                if at.n >= 2:
                    pool.wait_ge(rows_ready, at.times(SIZE, -SIZE))
                nc.gpsimd.tensor_tensor(var_eps[:, p, :], moments[:, p, :, 1],
                                        eps[:, :].to_broadcast([TOKENS, SIZE]), ALU.add).then_inc(var_ready, 1)
                pool.wait_ge(var_ready, at.times(1, 1))
                nc.gpsimd.tensor_tensor(rstd[:, p, :], var_eps[:, p, :], minus_half[:, :].to_broadcast([TOKENS, SIZE]),
                                        ALU.pow).then_inc(rstd_ready, 1)

            def residual(at):
                if at.n >= 2:
                    pool.wait_ge(out_added, at.times(1, -1))
                for k in range(SIZE):
                    row = base[:, at.n % 2, k, :]
                    if add_src:
                        nc.gpsimd.tensor_tensor(row, x[:, at.times(SIZE, k), :], src[:, at.times(SIZE, k), :],
                                                ALU.add).then_inc(base_sum, 1)
                        pool.wait_ge(base_sum, at.times(SIZE, k + 1))
                        nc.gpsimd.tensor_tensor(row, row, bias_out[:, :], ALU.add).then_inc(base_ready, 1)
                    else:
                        nc.gpsimd.tensor_tensor(row, x[:, at.times(SIZE, k), :], bias_out[:, :],
                                                ALU.add).then_inc(base_ready, 1)

            def step(t):
                if here(t, 3):
                    inverse_deviation(t.plus(3))
                if here(t, 1):
                    residual(t.plus(1))

            steps(pool, step)


def kernel(**inputs):
    import numpy as _np
    import concourse.bacc as _bacc
    from concourse import mybir as _mybir
    from concourse.bass_utils import run_bass_kernel_spmd as _run

    nc = _bacc.Bacc("TRN2", target_bir_lowering=False, num_devices=1)
    arrays, aps = {}, {}
    for name in inputs:
        value = _np.ascontiguousarray(inputs[name])
        arrays[f"in_{name}"] = value
        aps[name] = nc.dram_tensor(f"in_{name}", value.shape, _mybir.dt.from_np(value.dtype),
                                   kind="ExternalInput").ap()
    result = nc.dram_tensor("out_x", (BATCHES, TOKENS, DIM), _mybir.dt.float32, kind="ExternalOutput").ap()
    build(nc, aps, result)
    done = _run(nc, [arrays], core_ids=[0])
    return done.results[0]["out_x"]
```
